# Optimizing a Trainium2 kernel written in Bass

```python
import numpy as np
import jax
import jax.numpy as jnp

def _softmax(x, axis=-1):
    return jax.nn.softmax(x, axis=axis)

def _gelu(x):
    return jax.nn.gelu(x, approximate=True)

def _silu(x):
    return jax.nn.silu(x)

def _sigmoid(x):
    return jax.nn.sigmoid(x)

def _layernorm(x, axis=-1, eps=1e-05):
    m = jnp.mean(x, axis=axis, keepdims=True)
    v = jnp.var(x, axis=axis, keepdims=True)
    return (x - m) / jnp.sqrt(v + eps)

def _scatter_add(tgt, idx, src, axis=0):
    return tgt.at[idx].add(src)

def _segment_sum(src, seg, n):
    return jax.ops.segment_sum(src, seg, n)
kernel_name = 'mk_xattn_seq_d1_seqx_r4_28c815'

def setup_inputs(seed: int=0):
    np.random.seed(seed)
    _w = jnp.asarray

    def _rec_inputs():
        import jax
        import jax.numpy as jnp
        _rk = jax.random.key(seed)
        x = -0.0002928 + 1 * jax.random.normal(jax.random.fold_in(_rk, 1), (128, 128, 256), jnp.float32)
        _lenS = 128 - jax.random.randint(jax.random.fold_in(_rk, 7), (128,), 0, max(1, 128 // 4) + 1, jnp.int32)
        _lenS2 = 128 - jax.random.randint(jax.random.fold_in(_rk, 8), (128,), 0, max(1, 128 // 4) + 1, jnp.int32)
        _ctx_1024P = jax.random.normal(jax.random.fold_in(_rk, 11), (128, 16, 256), jnp.float32)
        _ctx_1024c = jax.random.dirichlet(jax.random.fold_in(_rk, 511), 0.3 * jnp.ones((16,), jnp.float32), (128, 128))
        _ctx_1024t = jnp.einsum('bsk,bkd->bsd', _ctx_1024c, _ctx_1024P)
        _ctx_1024t = _ctx_1024t * jax.lax.rsqrt(jnp.mean(jnp.square(_ctx_1024t)) + 1e-12) * 0.953939
        ctx_1024 = -1.39393e-06 + 0.999914 * (_ctx_1024t + 0.3 * jax.random.normal(jax.random.fold_in(_rk, 611), (128, 128, 256), jnp.float32))
        return (x, ctx_1024)
    x, ctx_1024 = _rec_inputs()

    def _L0_xattn_setup():
        import jax, jax.numpy as jnp
        import numpy as np
        D_MODEL = 256
        N_HEADS = 16
        D_K = D_MODEL // N_HEADS
        D_FF = 1024
        B, S = (2, 512)
        LN_EPS = 1e-05
        NEG_INF = -1e+30

        def layer_norm(x, g, b):
            mu = jnp.mean(x, axis=-1, keepdims=True)
            var = jnp.mean(jnp.square(x - mu), axis=-1, keepdims=True)
            return (x - mu) * jax.lax.rsqrt(var + LN_EPS) * g + b
        key = jax.random.key(seed)
        ks = jax.random.split(key, 16)
        sd = 0.02
        inp = {'query': jax.random.normal(ks[0], (B, S, D_MODEL), jnp.float32), 'key': jax.random.normal(ks[1], (B, S, D_MODEL), jnp.float32), 'values': jax.random.normal(ks[2], (B, S, D_MODEL), jnp.float32), 'Wq': jax.random.normal(ks[3], (D_MODEL, D_MODEL), jnp.float32) * sd, 'bq': jnp.zeros((D_MODEL,), jnp.float32), 'Wk': jax.random.normal(ks[4], (D_MODEL, D_MODEL), jnp.float32) * sd, 'bk': jnp.zeros((D_MODEL,), jnp.float32), 'Wv': jax.random.normal(ks[5], (D_MODEL, D_MODEL), jnp.float32) * sd, 'bv': jnp.zeros((D_MODEL,), jnp.float32), 'Wo': jax.random.normal(ks[6], (D_MODEL, D_MODEL), jnp.float32) * sd, 'bo': jnp.zeros((D_MODEL,), jnp.float32), 'ln1_g': jnp.ones((D_MODEL,), jnp.float32), 'ln1_b': jnp.zeros((D_MODEL,), jnp.float32), 'W1': jax.random.normal(ks[7], (D_MODEL, D_FF), jnp.float32) * sd, 'b1': jnp.zeros((D_FF,), jnp.float32), 'W2': jax.random.normal(ks[8], (D_FF, D_MODEL), jnp.float32) * sd, 'b2': jnp.zeros((D_MODEL,), jnp.float32), 'ln2_g': jnp.ones((D_MODEL,), jnp.float32), 'ln2_b': jnp.zeros((D_MODEL,), jnp.float32), 'mask': 0}
        return inp
    _L0_xattn_all = _L0_xattn_setup()
    _L0_xattn_in = {k: v for k, v in _L0_xattn_all.items() if k in ('Wq', 'bq', 'Wk', 'bk', 'Wv', 'bv', 'Wo', 'bo', 'ln1_g', 'ln1_b', 'W1', 'b1', 'W2', 'b2', 'ln2_g', 'ln2_b')}
    del _L0_xattn_all
    return {'x': x, 'ctx_1024': ctx_1024, 'L0_xattn_Wq': _L0_xattn_in['Wq'], 'L0_xattn_bq': _L0_xattn_in['bq'], 'L0_xattn_Wk': _L0_xattn_in['Wk'], 'L0_xattn_bk': _L0_xattn_in['bk'], 'L0_xattn_Wv': _L0_xattn_in['Wv'], 'L0_xattn_bv': _L0_xattn_in['bv'], 'L0_xattn_Wo': _L0_xattn_in['Wo'], 'L0_xattn_bo': _L0_xattn_in['bo'], 'L0_xattn_ln1_g': _L0_xattn_in['ln1_g'], 'L0_xattn_ln1_b': _L0_xattn_in['ln1_b'], 'L0_xattn_W1': _L0_xattn_in['W1'], 'L0_xattn_b1': _L0_xattn_in['b1'], 'L0_xattn_W2': _L0_xattn_in['W2'], 'L0_xattn_b2': _L0_xattn_in['b2'], 'L0_xattn_ln2_g': _L0_xattn_in['ln2_g'], 'L0_xattn_ln2_b': _L0_xattn_in['ln2_b']}

def reference(x, ctx_1024, L0_xattn_Wq, L0_xattn_bq, L0_xattn_Wk, L0_xattn_bk, L0_xattn_Wv, L0_xattn_bv, L0_xattn_Wo, L0_xattn_bo, L0_xattn_ln1_g, L0_xattn_ln1_b, L0_xattn_W1, L0_xattn_b1, L0_xattn_W2, L0_xattn_b2, L0_xattn_ln2_g, L0_xattn_ln2_b):
    import jax
    import jax.numpy as jnp

    def _L0_xattn_ref(query, key, values, Wq, bq, Wk, bk, Wv, bv, Wo, bo, ln1_g, ln1_b, W1, b1, W2, b2, ln2_g, ln2_b, mask):
        import jax, jax.numpy as jnp
        import numpy as np
        D_MODEL = 256
        N_HEADS = 16
        D_K = D_MODEL // N_HEADS
        D_FF = 1024
        B, S = (2, 512)
        LN_EPS = 1e-05
        NEG_INF = -1e+30

        def layer_norm(x, g, b):
            mu = jnp.mean(x, axis=-1, keepdims=True)
            var = jnp.mean(jnp.square(x - mu), axis=-1, keepdims=True)
            return (x - mu) * jax.lax.rsqrt(var + LN_EPS) * g + b
        b, s, d = query.shape
        q = (query @ Wq + bq).reshape(b, s, N_HEADS, D_K).transpose(0, 2, 1, 3)
        k = (key @ Wk + bk).reshape(b, s, N_HEADS, D_K).transpose(0, 2, 1, 3)
        v = (values @ Wv + bv).reshape(b, s, N_HEADS, D_K).transpose(0, 2, 1, 3)
        scores = jnp.einsum('bhqd,bhkd->bhqk', q, k) / jnp.sqrt(jnp.float32(D_K))
        i = jnp.arange(s)[:, None]
        j = jnp.arange(s)[None, :]
        allowed = j < i + mask
        scores = jnp.where(allowed, scores, NEG_INF)
        attn = jax.nn.softmax(scores, axis=-1)
        if mask == 0:
            attn = attn.at[:, :, 0, :].set(0.0)
        ctx = jnp.einsum('bhqk,bhkd->bhqd', attn, v)
        ctx = ctx.transpose(0, 2, 1, 3).reshape(b, s, d)
        attn_out = ctx @ Wo + bo
        x = layer_norm(query + attn_out, ln1_g, ln1_b)
        ffn = jax.nn.relu(x @ W1 + b1) @ W2 + b2
        out = layer_norm(x + ffn, ln2_g, ln2_b)
        return out
    x = _L0_xattn_ref(x, ctx_1024, ctx_1024, L0_xattn_Wq, L0_xattn_bq, L0_xattn_Wk, L0_xattn_bk, L0_xattn_Wv, L0_xattn_bv, L0_xattn_Wo, L0_xattn_bo, L0_xattn_ln1_g, L0_xattn_ln1_b, L0_xattn_W1, L0_xattn_b1, L0_xattn_W2, L0_xattn_b2, L0_xattn_ln2_g, L0_xattn_ln2_b, 0)
    return x

_drawn_inputs = setup_inputs


def setup_inputs(seed=0):
    import zlib

    import numpy as np

    out = dict(_drawn_inputs(seed))
    spreads = {'L0_xattn_bq': (0.0, 0.8),
     'L0_xattn_bk': (0.0, 0.8),
     'L0_xattn_bv': (0.0, 0.1),
     'L0_xattn_bo': (0.0, 0.1),
     'L0_xattn_ln1_g': (1.0, 0.2),
     'L0_xattn_ln1_b': (0.0, 0.1),
     'L0_xattn_b1': (0.0, 0.1),
     'L0_xattn_b2': (0.0, 0.1),
     'L0_xattn_ln2_g': (1.0, 0.2),
     'L0_xattn_ln2_b': (0.0, 0.1)}
    factors = {'L0_xattn_Wq': 8.0, 'L0_xattn_Wk': 8.0}
    for name, (base, spread) in spreads.items():
        noise = np.random.default_rng([zlib.crc32(name.encode()), seed]).standard_normal(out[name].shape)
        drawn = base * np.exp(spread * noise) if base else spread * noise
        out[name] = jnp.asarray(drawn.astype(out[name].dtype))
    for name, factor in factors.items():
        out[name] = (out[name] * factor).astype(out[name].dtype)
    return out
```

```python
from contextlib import ExitStack

import concourse.bass as bass
from concourse import mybir

F32 = mybir.dt.float32
F32R = mybir.dt.float32r
BF16 = mybir.dt.bfloat16
ALU = mybir.AluOpType
ACT = mybir.ActivationFunctionType
AX = mybir.AxisListType

P = 128
B, S, D = 128, 128, 256
H, DK = 16, 16
FF = 1024
KC = D // P
FC = FF // P
GB = 2
NG = B // GB
GT = GB * S
PAIRS = H // 2
UNITS = GB * 4
LN_EPS = 1e-5
MASKED = -1e30
PARTS = 3
QPART = (0, 0, 1)
KPART = (0, 1, 0)
SPLIT = ((0, 0), (0, 1), (1, 0))
FIRST, LAST = 4, NG - 3


def exists(g):
    return 0 <= g < NG if isinstance(g, int) else True


def need(eng, sem, value):
    if not isinstance(value, int) or value > 0:
        eng.wait_ge(sem, value)


def count(eng, value):
    return value if isinstance(value, int) else eng.snap(value)


def lagged(it, slot, lag):
    m = slot - lag
    return (it, m) if m >= 0 else (it - 1, m + UNITS)


def run(eng, iteration):
    for it in range(-1, FIRST):
        iteration(it, it % 2)
    with eng.Fori(FIRST, LAST, 2) as it:
        iteration(it, 0)
        iteration(it + 1, 1)
    for it in range(LAST + 1, NG + 3):
        iteration(it, it % 2)


def encoder_layer(nc, x, ctx_in, Wq, bq, Wk, bk, Wv, bv, Wo, bo, ln1_g, ln1_b, W1, b1, W2, b2, ln2_g, ln2_b, out):
    ctx = ExitStack()
    with ctx:
        def sb(name, shape, dt=F32):
            return ctx.enter_context(nc.sbuf_tensor(name, shape, dt))

        def psum(name, shape):
            return ctx.enter_context(nc.psum_tensor(name, shape, F32))

        def sem(name):
            return ctx.enter_context(nc.semaphore(name))

        x_v = x.rearrange("(g b) s d -> g s b d", b=GB)
        c_v = ctx_in.rearrange("(g b) s d -> g s b d", b=GB)
        out_v = out.rearrange("(g b) s d -> g s b d", b=GB)

        wq = sb("wq", [P, 2, KC, D], F32R)
        wk = sb("wk", [P, 2, KC, D], F32R)
        wv = sb("wv", [P, 2, KC, D], F32R)
        wo = sb("wo", [P, 2, KC, D], F32R)
        w1 = sb("w1", [P, 2, KC, FF], F32R)
        w2 = sb("w2", [P, 2, FC, D], F32R)
        bq_col = sb("bq_col", [P, KC])
        bk_col = sb("bk_col", [P, KC])
        b1_col = sb("b1_col", [P, FC])
        bv_row = sb("bv_row", [P, GB, D])
        bo_row = sb("bo_row", [P, D])
        g1_row = sb("g1_row", [P, D])
        be1_row = sb("be1_row", [P, D])
        b2_row = sb("b2_row", [P, D])
        g2_row = sb("g2_row", [P, D])
        be2_row = sb("be2_row", [P, D])
        ident = sb("ident", [P, P])
        ident_bf = sb("ident_bf", [P, P], BF16)
        mask_f = sb("mask_f", [P, P])
        mask_bf = sb("mask_bf", [P, P], BF16)
        not_first = sb("not_first", [P, 1])
        neg_half = sb("neg_half", [P, GB])
        of_head = sb("of_head", [P, 2])

        x_tok = sb("x_tok", [P, GB, D])
        c_tok = sb("c_tok", [P, GB, D])
        x_res = sb("x_res", [P, GB, D])
        xT = sb("xT", [P, 2, KC, GT], F32R)
        cT = sb("cT", [P, 2, KC, GT], F32R)
        qT = sb("qT", [P, 2, KC, GT], F32R)
        kT = sb("kT", [P, 2, KC, GT], F32R)
        k_head = sb("k_head", [P, 2, KC, 2, GT], F32R)
        q_stack = [sb(f"q_stack{i}", [PARTS * 32, 4, KC, GT], F32R) for i in range(2)]
        k_stack = [sb(f"k_stack{i}", [PARTS * 32, 4, KC, 2, GT], F32R) for i in range(2)]
        v_sb = sb("v_sb", [P, GB, PAIRS, 3, DK])
        probs = sb("probs", [P, 4, 4, S])
        probsT = sb("probsT", [P, 4, 4, S])
        negmax = sb("negmax", [P, 4, 4])
        sums = sb("sums", [P, 4, 4])
        recip = sb("recip", [P, 4, 4])
        scale_p = sb("scale_p", [P, 4, 4])
        aT = sb("aT", [P, 2, KC, GT], F32R)
        u1 = sb("u1", [P, GB, D])
        y = sb("y", [P, GB, D])
        y_b2 = sb("y_b2", [P, GB, D])
        yT = sb("yT", [P, 2, KC, GT], F32R)
        hT = sb("hT", [P, 2, FC, GT], F32R)
        h_full = sb("h_full", [P, 2, 2, GT])
        u2 = sb("u2", [P, GB, D])
        o_tok = sb("o_tok", [P, GB, D])
        stats = sb("stats", [P, 2, GB, 6])
        mv = sb("mv", [P, 2, GB, 2])
        var_eps = sb("var_eps", [P, 2, GB])
        rstd = sb("rstd", [P, 2, GB])

        ps_scores = [psum(f"ps_scores{i}", [P, 4, S]) for i in range(2)]
        ps_probsT = [psum(f"ps_probsT{i}", [P, 4, S]) for i in range(2)]
        ps_att = psum("ps_att", [P, 512])
        ps_dense = [psum(f"ps_dense{i}", [P, 512]) for i in range(3)]

        ORDER = ["f1_0", "f1_1", "f1_2", "xT", "f1_3", "v", "wo", "cT", "q", "f2", "k", "yT"]
        BANK = {"f1_0": 1, "f1_1": 2, "f1_2": 1, "xT": 0, "f1_3": 2, "v": 1, "wo": 0, "cT": 2, "q": 1,
                "f2": 0, "k": 2, "yT": 1}
        OFFSET = {"f1_0": -2, "f1_1": -2, "f1_2": -2, "xT": 1, "f1_3": -2, "v": 0, "wo": -1, "cT": 1, "q": 1,
                  "f2": -2, "k": 1, "yT": -1}
        full = {n: sem(f"{n}_full") for n in ORDER}
        taken = {n: sem(f"{n}_taken") for n in ORDER}
        TAKES = {"f1_0": 2, "f1_1": 2, "f1_2": 2, "f1_3": 2, "xT": 1, "cT": 1, "yT": 1, "q": 2, "k": 2,
                 "v": 1, "wo": 1, "f2": 1}

        s_w = [sem(f"weight_loaded{i}") for i in range(2)]
        s_wc = sem("columns_loaded")
        s_wr = sem("rows_loaded")
        s_wscaled = sem("wq_scaled")
        s_whi = sem("weights_hi")
        s_wlo = sem("weights_lo")
        s_zero = sem("consts_zeroed")
        s_const = sem("consts_ready")
        s_cbf = sem("consts_bf_ready")
        s_x = sem("x_loaded")
        s_c = sem("c_loaded")
        s_xres = sem("x_res_loaded")
        s_xb = sem("x_res_plus_bo")
        s_hi = {n: sem(f"{n}_hi") for n in ("xT", "cT", "q", "k", "yT", "att", "f1")}
        s_khead = sem("k_head_ready")
        s_qstack = sem("q_stacked")
        s_kstack = sem("k_stacked")
        s_scores = sem("scores_ready")
        s_max = sem("max_ready")
        s_exp = sem("exp_ready")
        s_recip = sem("recip_ready")
        s_scale = sem("scale_ready")
        s_norm = sem("probs_normalised")
        s_pT = sem("probsT_full")
        s_pTsb_a = sem("probsT_taken_act")
        s_pTsb_v = sem("probsT_taken_dve")
        s_att = sem("att_ready")
        s_att_lo = sem("att_taken")
        s_st1 = sem("stats1_ready")
        s_mv1 = sem("meanvar1_ready")
        s_ve1 = sem("var_eps1_ready")
        s_rs1 = sem("rstd1_ready")
        s_z1 = sem("z1_ready")
        s_y0 = sem("y_scaled")
        s_y = sem("y_ready")
        s_yb = sem("y_b2_ready")
        s_hfull = sem("h_full_ready")
        s_hlo = sem("h_lo_ready")
        s_st2 = sem("stats2_ready")
        s_mv2 = sem("meanvar2_ready")
        s_ve2 = sem("var_eps2_ready")
        s_rs2 = sem("rstd2_ready")
        s_z2 = sem("z2_ready")
        s_o0 = sem("o_scaled")
        s_o = sem("o_ready")
        s_out = sem("out_stored")

        WEIGHTS = [(Wq, wq, KC, D), (Wk, wk, KC, D), (Wv, wv, KC, D), (Wo, wo, KC, D), (W1, w1, KC, FF),
                   (W2, w2, FC, D)]
        w_raw = [t[:].rearrange("p u h k -> p (u h k)") for t in (probs, probsT)]
        raws = [w_raw[i % 2][:, 0:c * n].rearrange("p (c n) -> p c n", c=c)
                for i, (_, _, c, n) in enumerate(WEIGHTS)]
        ROWS = [(bv, bv_row[:, b, :]) for b in range(GB)] + [
            (bo, bo_row[:]), (ln1_g, g1_row[:]), (ln1_b, be1_row[:]), (b2, b2_row[:]), (ln2_g, g2_row[:]),
            (ln2_b, be2_row[:])]
        COLS = [(bq, bq_col), (bk, bk_col), (b1, b1_col)]

        def f32(ap):
            return ap.bitcast(F32)

        block = ctx.enter_context(nc.Block())

        @block.sync
        def _(sp):
            for dram, tile in COLS:
                sp.dma_start(tile[:], dram.rearrange("(c p) -> p c", p=P), allow_slow_non_contiguous=True).then_inc(s_wc, 16)
            for dram, tile in ROWS:
                sp.dma_start(tile, dram.rearrange("(a n) -> a n", a=1).broadcast_to([P, D])).then_inc(s_wr, 16)

            def iteration(it, odd):
                x_free = count(sp, it + 2)
                out_due = count(sp, it - 2)
                res_free = count(sp, it)
                scores_done = count(sp, it * UNITS)
                q_taken = count(sp, it * KC + 2 * KC)
                k_ready = count(sp, it * 4 + 8)
                g = it + 2
                if exists(g):
                    need(sp, full["xT"], x_free)
                    sp.dma_start(x_tok[:], x_v[g]).then_inc(s_x, 16)
                g = it - 3
                if exists(g):
                    need(sp, s_o, out_due)
                    sp.dma_start(out_v[g], o_tok[:]).then_inc(s_out, 16)
                g = it
                if exists(g):
                    need(sp, taken["wo"], res_free)
                    sp.dma_start(x_res[:], x_v[g]).then_inc(s_xres, 16)
                g = it + 2
                if exists(g):
                    need(sp, full["cT"], x_free)
                    sp.dma_start(c_tok[:], c_v[g]).then_inc(s_c, 16)
                g = it + 1
                if exists(g):
                    need(sp, s_scores, scores_done)
                    need(sp, taken["q"], q_taken)
                    for s, half in enumerate(QPART):
                        for j in range(4):
                            sp.dma_start(f32(q_stack[1 - odd][32 * s:32 * s + 32, j]),
                                         f32(qT[32 * j:32 * j + 32, half])).then_inc(s_qstack, 16)
                    need(sp, s_khead, k_ready)
                    for s, half in enumerate(KPART):
                        for j in range(4):
                            sp.dma_start(f32(k_stack[1 - odd][32 * s:32 * s + 32, j]),
                                         f32(k_head[32 * j:32 * j + 32, half]))\
                              .then_inc(s_kstack, 16)

            sp.dma_start(x_tok[:], x_v[0]).then_inc(s_x, 16)
            sp.dma_start(c_tok[:], c_v[0]).then_inc(s_c, 16)
            for i, ((dram, _, c, _), raw) in enumerate(zip(WEIGHTS, raws)):
                need(sp, s_wlo, i - 1)
                sp.dma_start(raw, dram.rearrange("(c p) n -> p c n", p=P)).then_inc(s_w[i % 2], 16)
            run(sp, iteration)
            sp.wait_ge(s_out, 16 * NG)

        @block.tensor
        def _(pe):
            pe.wait_ge(s_const, 3)
            pe.wait_ge(s_cbf, 2)
            pe.wait_ge(s_wlo, len(WEIGHTS))
            pe.wait_ge(s_whi, len(WEIGHTS))

            def bank_free(it, name):
                n = ORDER.index(name)
                for back in range(1, 2 * len(ORDER)):
                    i, m = (it, n - back) if back <= n else (it - 1, n - back + len(ORDER))
                    if m < 0:
                        return
                    prev = ORDER[m]
                    g = i + OFFSET[prev]
                    if BANK[prev] == BANK[name] and exists(g):
                        need(pe, taken[prev], (g + 1) * TAKES[prev])
                        return

            def transposes(it, name, src):
                bank_free(it, name)
                for c in range(KC):
                    for b in range(GB):
                        last = nc.tensor.transpose(
                            ps_dense[BANK[name]][:, c * GT + b * S:c * GT + (b + 1) * S],
                            src[:, b, c * P:(c + 1) * P], ident[:])
                last.then_inc(full[name], 1)

            def columns_product(it, name, w, acts, chunks):
                bank_free(it, name)
                for i, ch in enumerate(chunks):
                    steps = [(kc, a, c) for kc in range(KC) for a, c in SPLIT]
                    for n, (kc, a, c) in enumerate(steps):
                        last = nc.tensor.matmul(ps_dense[BANK[name]][:, i * GT:(i + 1) * GT],
                                                w[:, a, kc, ch * P:(ch + 1) * P], acts[:, c, kc, :],
                                                start=(n == 0), stop=(n == len(steps) - 1))
                last.then_inc(full[name], 1)

            def tokens_product(name, w, acts, b, kcs, total):
                for kc in kcs:
                    for n, (a, c) in enumerate(SPLIT):
                        last = nc.tensor.matmul(ps_dense[BANK[name]][:, b * D:(b + 1) * D],
                                                acts[:, a, kc, b * S:(b + 1) * S], w[:, c, kc, :],
                                                start=(kc == 0 and n == 0),
                                                stop=(kc == total - 1 and n == len(SPLIT) - 1))
                return last

            def x_transpose(it):
                g = it + 1
                if exists(g):
                    pe.wait_ge(s_x, 16 * (g + 1))
                    transposes(it, "xT", x_tok)

            def c_transpose(it):
                g = it + 1
                if exists(g):
                    pe.wait_ge(s_c, 16 * (g + 1))
                    transposes(it, "cT", c_tok)

            def y_transpose(it):
                g = it - 1
                if exists(g):
                    pe.wait_ge(s_y, g + 1)
                    transposes(it, "yT", y)

            def q_project(it):
                g = it + 1
                if exists(g):
                    pe.wait_ge(taken["xT"], g + 1)
                    columns_product(it, "q", wq, xT, range(KC))

            def k_project(it):
                g = it + 1
                if exists(g):
                    pe.wait_ge(taken["cT"], g + 1)
                    columns_product(it, "k", wk, cT, range(KC))

            def v_project(it):
                g = it
                if exists(g):
                    bank_free(it, "v")
                    for b in range(GB):
                        last = tokens_product("v", wv, cT, b, range(KC), KC)
                    last.then_inc(full["v"], 1)

            def out_project(it):
                g = it - 1
                if exists(g):
                    pe.wait_ge(s_att_lo, GB * (g + 1))
                    bank_free(it, "wo")
                    for b in range(GB):
                        last = tokens_product("wo", wo, aT, b, range(KC), KC)
                    last.then_inc(full["wo"], 1)

            def ff_up(n):
                def part(it):
                    g = it - 2
                    if exists(g):
                        pe.wait_ge(taken["yT"], g + 1)
                        columns_product(it, f"f1_{n}", w1, yT, (2 * n, 2 * n + 1))
                return part

            def ff_down(q):
                def part(it):
                    g = it - 2
                    if exists(g):
                        if q == 0:
                            bank_free(it, "f2")
                        b, half = q // 2, q % 2
                        pe.wait_ge(s_hlo, 4 * g + 2 * (half + 1))
                        last = tokens_product("f2", w2, hT, b, range(4 * half, 4 * half + 4), FC)
                        if q == 3:
                            last.then_inc(full["f2"], 1)
                return part

            def scores(it, slot, odd):
                g, m = it, slot
                if not exists(g):
                    return
                b, w = m // 4, m % 4
                if m == 0:
                    pe.wait_ge(s_qstack, 16 * 4 * PARTS * (g + 1))
                    pe.wait_ge(s_kstack, 16 * 4 * PARTS * (g + 1))
                need(pe, s_exp, g * UNITS + m - 1)
                bank = ps_scores[m % 2]
                nc.tensor.matmul(bank[:], ident_bf[:], mask_bf[:].unsqueeze(1).broadcast_to([P, 4, S]),
                                 start=True, stop=False, skip_group_check=True)
                for i in range(2):
                    c, j = w // 2, 2 * (w % 2) + i
                    last = nc.tensor.matmul(bank[:, 2 * i:2 * i + 2, :], q_stack[odd][:, j, c, b * S:(b + 1) * S],
                                            k_stack[odd][:, j, c, :, b * S:(b + 1) * S], start=False, stop=(i == 1),
                                            skip_group_check=True)
                last.then_inc(s_scores, 1)

            def probs_transpose(it, slot):
                g, m = lagged(it, slot, 2)
                if not exists(g):
                    return
                pe.wait_ge(s_norm, g * UNITS + m + 1)
                need(pe, (s_pTsb_a, s_pTsb_v)[m % 2], g * (UNITS // 2) + m // 2)
                for i in range(4):
                    last = nc.tensor.transpose(ps_probsT[m % 2][:, i, :], probs[:, m % 4, i, :], ident[:])
                last.then_inc(s_pT, 1)

            def attend(it, slot):
                g, m = lagged(it, slot, 3)
                if m % 2 == 0 or not exists(g):
                    return
                b, c = m // 4, (m % 4) // 2
                pe.wait_ge(s_pTsb_a, g * (UNITS // 2) + m // 2 + 1)
                pe.wait_ge(s_pTsb_v, g * (UNITS // 2) + m // 2 + 1)
                if m == 1:
                    pe.wait_ge(taken["v"], g + 1)
                if c == 0:
                    need(pe, s_att_lo, g * GB + b)
                for e in range(2):
                    for j in range(4):
                        unit = (m - 1 + j // 2) % 4
                        last = nc.tensor.matmul(
                            ps_att[32 * j:32 * j + 32, c * S:(c + 1) * S],
                            v_sb[:, b, 4 * c + j, e:e + 2, :],
                            probsT[:, unit, 2 * (j % 2) + e, :],
                            start=(e == 0), stop=(e == 1), tile_position=(0, 32 * j), skip_group_check=True)
                last.then_inc(s_att, 1)

            DENSE = [([ff_up(0)], [ff_up(1)]),
                     ([ff_up(2)], [x_transpose]),
                     ([ff_up(3)], []),
                     ([out_project, c_transpose], [q_project]),
                     ([ff_down(0)], [k_project]),
                     ([ff_down(1)], []),
                     ([ff_down(2)], [y_transpose]),
                     ([ff_down(3)], [])]

            def iteration(it, odd):
                for slot in range(UNITS):
                    scores(it, slot, odd)
                    for part in DENSE[slot][0]:
                        part(it)
                    probs_transpose(it, slot)
                    for part in DENSE[slot][1]:
                        part(it)
                    attend(it, slot)
                    if slot == 2:
                        v_project(it)

            run(pe, iteration)

        @block.scalar
        def _(act):
            act.wait_ge(s_wc, 16 * len(COLS))
            act.wait_ge(s_wscaled, 2)

            def exponentials(it, slot):
                g, m = it, slot
                if not exists(g):
                    return
                act.wait_ge(s_max, g * UNITS + m + 1)
                need(act, s_pT, g * UNITS + m - 3)
                need(act, s_scale, g * UNITS + m - 3)
                for i in range(4):
                    last = nc.scalar.activation(probs[:, m % 4, i, :], ps_scores[m % 2][:, i, :], ACT.Exp,
                                                bias=negmax[:, m % 4, i:i + 1],
                                                accum_out=sums[:, m % 4, i:i + 1])
                last.then_inc(s_exp, 1)

            def take_probsT(it, slot):
                g, m = lagged(it, slot, 2)
                if m % 2 or not exists(g):
                    return
                act.wait_ge(s_pT, g * UNITS + m + 1)
                need(act, s_att, (g * UNITS + m) // 2 - 1 if isinstance(g, int) else g * (UNITS // 2) + m // 2 - 1)
                nc.scalar.activation(probsT[:, m % 4, :, :], ps_probsT[m % 2][:], ACT.Copy).then_inc(s_pTsb_a, 1)

            def take_hi(name, src, dst, g, reader, count):
                act.wait_ge(full[name], g + 1)
                need(act, reader, count)
                nc.scalar.activation(dst, src, ACT.Copy).then_inc(s_hi[name], 1)

            def x_hi(it):
                g = it + 1
                if exists(g):
                    take_hi("xT", ps_dense[BANK["xT"]][:], xT[:, 0].rearrange("p c t -> p (c t)"), g, full["q"], g)

            def c_hi(it):
                g = it + 1
                if exists(g):
                    take_hi("cT", ps_dense[BANK["cT"]][:], cT[:, 0].rearrange("p c t -> p (c t)"), g, full["v"], g)

            def y_hi(it):
                g = it - 1
                if exists(g):
                    take_hi("yT", ps_dense[BANK["yT"]][:], yT[:, 0].rearrange("p c t -> p (c t)"), g,
                            full["f1_3"], g)

            def qk_hi(name, dst, bias, reader, per):
                def part(it):
                    g = it + 1
                    if exists(g):
                        act.wait_ge(full[name], g + 1)
                        need(act, reader, per * g)
                        for c in range(KC):
                            nc.scalar.activation(dst[:, 0, c, :], ps_dense[BANK[name]][:, c * GT:(c + 1) * GT],
                                                 ACT.Identity, bias=bias[:, c:c + 1]).then_inc(s_hi[name], 1)
                return part

            def h_relu(n):
                def part(it):
                    g = it - 2
                    if exists(g):
                        name = f"f1_{n}"
                        act.wait_ge(s_hi["f1"], 8 * g + 2 * (n + 1))
                        need(act, s_hlo, 4 * g + n - 1)
                        for i in range(2):
                            nc.scalar.activation(h_full[:, n % 2, i, :], ps_dense[BANK[name]][:, i * GT:(i + 1) * GT],
                                                 ACT.Relu, bias=b1_col[:, 2 * n + i:2 * n + i + 1])\
                              .then_inc(taken[name], 1)
                return part

            def att_hi(it, slot):
                g, m = lagged(it, slot, 3)
                if m % 4 != 3 or not exists(g):
                    return
                b = m // 4
                act.wait_ge(s_att, (g * GB + b + 1) * 2)
                need(act, full["wo"], g)
                nc.scalar.activation(aT[:, 0, :, b * S:(b + 1) * S],
                                     ps_att[:, 0:KC * S].rearrange("p (c t) -> p c t", c=KC), ACT.Copy)\
                  .then_inc(s_hi["att"], 1)

            DENSE = [([h_relu(0)], [h_relu(1)]),
                     ([h_relu(2)], [x_hi]),
                     ([h_relu(3)], []),
                     ([c_hi], [qk_hi("q", qT, bq_col, s_qstack, 16 * 4 * PARTS)]),
                     ([], [qk_hi("k", kT, bk_col, s_khead, 4)]),
                     ([], []),
                     ([], [y_hi]),
                     ([], [])]

            def iteration(it, odd):
                for slot in range(UNITS):
                    exponentials(it, slot)
                    for part in DENSE[slot][0]:
                        part(it)
                    take_probsT(it, slot)
                    for part in DENSE[slot][1]:
                        part(it)
                    att_hi(it, slot)

            run(act, iteration)

        @block.vector
        def _(dve):
            dve.wait_ge(s_wc, 16 * len(COLS))
            nc.vector.tensor_scalar(bq_col[:], bq_col[:], float(DK) ** -0.5, None, ALU.mult).then_inc(s_wscaled, 1)
            for i, ((_, w, _, _), raw) in enumerate(zip(WEIGHTS, raws)):
                dve.wait_ge(s_w[i % 2], 16 * (i // 2 + 1))
                if i == 0:
                    nc.vector.tensor_scalar(raw, raw, float(DK) ** -0.5, None, ALU.mult).then_inc(s_wscaled, 1)
                    dve.wait_ge(s_wscaled, 2)
                nc.vector.tensor_copy(w[:, 0], raw).then_inc(s_whi, 1)
                dve.wait_ge(s_whi, i + 1)
                nc.vector.tensor_tensor(w[:, 1], raw, f32(w[:, 0]), ALU.subtract).then_inc(s_wlo, 1)
            dve.wait_ge(s_const, 3)
            nc.vector.tensor_copy(ident_bf[:], ident[:]).then_inc(s_cbf, 1)
            nc.vector.tensor_copy(mask_bf[:], mask_f[:]).then_inc(s_cbf, 1)
            for e in range(2):
                nc.vector.tensor_reduce(of_head[:, e:e + 1],
                                        ident[:].rearrange("p (j e d) -> p e j d", j=4, e=2)[:, e], AX.XY, ALU.add)\
                  .then_inc(s_cbf, 1)
            dve.wait_ge(s_cbf, 4)
            dve.wait_ge(s_wr, 16 * len(ROWS))

            def maxima(it, slot):
                g, m = it, slot
                if not exists(g):
                    return
                dve.wait_ge(s_scores, g * UNITS + m + 1)
                need(dve, s_exp, g * UNITS + m - 3)
                nc.vector.tensor_reduce(negmax[:, m % 4, :], ps_scores[m % 2][:], AX.X, ALU.max, negate=True)\
                  .then_inc(s_max, 1)

            def reciprocals(it, slot):
                g, m = lagged(it, slot, 1)
                if not exists(g):
                    return
                U = g * UNITS + m
                dve.wait_ge(s_exp, U + 1)
                need(dve, s_norm, U - 3)
                nc.vector.reciprocal(recip[:, m % 4, :], sums[:, m % 4, :]).then_inc(s_recip, 1)
                dve.wait_ge(s_recip, U + 1)
                nc.vector.tensor_scalar(scale_p[:, m % 4, :], recip[:, m % 4, :], not_first[:], None, ALU.mult)\
                  .then_inc(s_scale, 1)

            def take_probsT(it, slot):
                g, m = lagged(it, slot, 2)
                if m % 2 == 0 or not exists(g):
                    return
                dve.wait_ge(s_pT, g * UNITS + m + 1)
                need(dve, s_att, g * (UNITS // 2) + m // 2 - 1)
                nc.vector.tensor_copy(probsT[:, m % 4, :, :], ps_probsT[m % 2][:]).then_inc(s_pTsb_v, 1)

            def take_lo(name, src, dst, g):
                dve.wait_ge(s_hi[name], g + 1)
                nc.vector.tensor_tensor(dst[:, 1].rearrange("p c t -> p (c t)"), src,
                                        f32(dst[:, 0].rearrange("p c t -> p (c t)")), ALU.subtract)\
                  .then_inc(taken[name], 1)

            def x_lo(it):
                if exists(it + 1):
                    take_lo("xT", ps_dense[BANK["xT"]][:], xT, it + 1)

            def c_lo(it):
                if exists(it + 1):
                    take_lo("cT", ps_dense[BANK["cT"]][:], cT, it + 1)

            def y_lo(it):
                if exists(it - 1):
                    take_lo("yT", ps_dense[BANK["yT"]][:], yT, it - 1)

            def qk_lo(name, dst, bias):
                def part(it):
                    g = it + 1
                    if exists(g):
                        dve.wait_ge(s_hi[name], (g + 1) * KC)
                        for c in range(KC):
                            nc.vector.scalar_tensor_tensor(
                                out=dst[:, 1, c, :], in0=ps_dense[BANK[name]][:, c * GT:(c + 1) * GT],
                                scalar=bias[:, c:c + 1], in1=f32(dst[:, 0, c, :]), op0=ALU.add,
                                op1=ALU.subtract).then_inc(taken[name], 1)
                return part

            def k_separate(it):
                g = it + 1
                if exists(g):
                    dve.wait_ge(taken["k"], (g + 1) * KC)
                    need(dve, s_kstack, 16 * 4 * PARTS * g)
                    for half in range(2):
                        for e in range(2):
                            nc.vector.tensor_scalar(k_head[:, half, :, e, :], f32(kT[:, half]),
                                                    of_head[:, e:e + 1], None, ALU.mult).then_inc(s_khead, 1)

            def take_v(it):
                g = it
                if exists(g):
                    dve.wait_ge(full["v"], g + 1)
                    need(dve, s_att, g * (UNITS // 2))
                    if isinstance(g, int) and g == 0:
                        dve.wait_ge(s_zero, 5)
                    nc.vector.tensor_tensor(
                        v_sb[:].rearrange("p b h e d -> p (b h) e d")[:, :, 0:3:2, :],
                        ps_dense[BANK["v"]][:].rearrange("p (b h e d) -> p (b h) e d", b=GB, h=PAIRS, e=2),
                        bv_row[:].rearrange("p b (h e d) -> p (b h) e d", h=PAIRS, e=2), ALU.add)\
                      .then_inc(taken["v"], 1)

            def h_hi(n):
                def part(it):
                    g = it - 2
                    if exists(g):
                        name = f"f1_{n}"
                        dve.wait_ge(full[name], g + 1)
                        need(dve, full["f2"], g)
                        for i in range(2):
                            nc.vector.tensor_scalar(hT[:, 0, 2 * n + i, :], ps_dense[BANK[name]][:, i * GT:(i + 1) * GT],
                                                    b1_col[:, 2 * n + i:2 * n + i + 1], 0.0, ALU.add, ALU.max)\
                              .then_inc(s_hi["f1"], 1)
                return part

            def att_lo(it, slot):
                g, m = lagged(it, slot, 3)
                if m % 4 != 3 or not exists(g):
                    return
                b = m // 4
                dve.wait_ge(s_hi["att"], g * GB + b + 1)
                nc.vector.tensor_tensor(aT[:, 1, :, b * S:(b + 1) * S],
                                        ps_att[:, 0:KC * S].rearrange("p (c t) -> p c t", c=KC),
                                        f32(aT[:, 0, :, b * S:(b + 1) * S]), ALU.subtract).then_inc(s_att_lo, 1)

            def statistics(n, u, g, s_u, s_st):
                dve.wait_ge(s_u, g + 1)
                for b in range(GB):
                    nc.vector.bn_stats(stats[:, n, b, :], u[:, b, :]).then_inc(s_st, 1)

            def mean_variance(n, g, s_mv, s_ve):
                for b in range(GB):
                    nc.vector.bn_aggr(mv[:, n, b, :], stats[:, n, b, :]).then_inc(s_mv, 1)
                dve.wait_ge(s_mv, GB * (g + 1))
                nc.vector.tensor_scalar(var_eps[:, n, :], mv[:, n, :, 1], LN_EPS, None, ALU.add).then_inc(s_ve, 1)

            def standardise(n, u, g, s_rs, s_z):
                dve.wait_ge(s_rs, g + 1)
                for b in range(GB):
                    nc.vector.tensor_scalar(u[:, b, :], u[:, b, :], mv[:, n, b, 0:1], rstd[:, n, b:b + 1],
                                            ALU.subtract, ALU.mult).then_inc(s_z, 1)

            def norm1_stats(it):
                g = it - 1
                if exists(g):
                    dve.wait_ge(full["wo"], g + 1)
                    dve.wait_ge(s_xb, g + 1)
                    need(dve, s_y0, g)
                    nc.vector.tensor_tensor(u1[:].rearrange("p b d -> p (b d)"), ps_dense[BANK["wo"]][:],
                                            x_res[:].rearrange("p b d -> p (b d)"), ALU.add)\
                      .then_inc(taken["wo"], 1)
                    statistics(0, u1, g, taken["wo"], s_st1)
                    dve.wait_ge(s_st1, GB * (g + 1))
                c_lo(it)
                if exists(g):
                    mean_variance(0, g, s_mv1, s_ve1)

            def norm1(it):
                if exists(it - 1):
                    standardise(0, u1, it - 1, s_rs1, s_z1)

            def norm2_stats(it):
                g = it - 2
                if exists(g):
                    dve.wait_ge(full["f2"], g + 1)
                    dve.wait_ge(s_yb, g + 1)
                    need(dve, s_o0, g)
                    nc.vector.tensor_tensor(u2[:].rearrange("p b d -> p (b d)"), ps_dense[BANK["f2"]][:],
                                            y_b2[:].rearrange("p b d -> p (b d)"), ALU.add)\
                      .then_inc(taken["f2"], 1)
                    statistics(1, u2, g, taken["f2"], s_st2)

            def norm2(it):
                if exists(it - 3):
                    standardise(1, u2, it - 3, s_rs2, s_z2)

            DENSE = [([norm2, h_hi(0)], [h_hi(1)]),
                     ([h_hi(2)], [x_lo]),
                     ([h_hi(3)], []),
                     ([norm1_stats], [qk_lo("q", qT, bq_col)]),
                     ([norm1], [qk_lo("k", kT, bk_col), k_separate]),
                     ([], []),
                     ([], [y_lo]),
                     ([], [norm2_stats])]

            def iteration(it, odd):
                for slot in range(UNITS):
                    if slot == 0 and exists(it - 3):
                        dve.wait_ge(s_st2, GB * (it - 2))
                    maxima(it, slot)
                    if slot == 0 and exists(it - 3):
                        mean_variance(1, it - 3, s_mv2, s_ve2)
                    reciprocals(it, slot)
                    for part in DENSE[slot][0]:
                        part(it)
                    take_probsT(it, slot)
                    for part in DENSE[slot][1]:
                        part(it)
                    att_lo(it, slot)
                    if slot == 2:
                        take_v(it)

            run(dve, iteration)

        @block.gpsimd
        def _(pool):
            nc.gpsimd.memset(v_sb[:], 0.0).then_inc(s_zero, 1)
            nc.gpsimd.memset(ident[:], 0.0).then_inc(s_zero, 1)
            nc.gpsimd.memset(mask_f[:], 0.0).then_inc(s_zero, 1)
            nc.gpsimd.memset(not_first[:], 1.0).then_inc(s_zero, 1)
            nc.gpsimd.memset(neg_half[:], -0.5).then_inc(s_zero, 1)
            pool.wait_ge(s_zero, 5)
            nc.gpsimd.affine_select(out=ident[:], in_=ident[:], compare_op=ALU.not_equal, fill=1.0, base=0,
                                    pattern=[[-1, P]], channel_multiplier=1).then_inc(s_const, 1)
            nc.gpsimd.affine_select(out=mask_f[:], in_=mask_f[:], compare_op=ALU.is_gt, fill=MASKED, base=0,
                                    pattern=[[-1, P]], channel_multiplier=1).then_inc(s_const, 1)
            nc.gpsimd.affine_select(out=not_first[:], in_=not_first[:], compare_op=ALU.not_equal, fill=0.0, base=0,
                                    pattern=[[0, 1]], channel_multiplier=1).then_inc(s_const, 1)
            pool.wait_ge(s_const, 3)
            pool.wait_ge(s_wr, 16 * len(ROWS))

            def row(tile):
                return tile[:].unsqueeze(1).broadcast_to([P, GB, D])

            def normalise(it, slot):
                g, m = lagged(it, slot, 1)
                if not exists(g):
                    return
                pool.wait_ge(s_scale, g * UNITS + m + 1)
                pool.wait_ge(s_exp, g * UNITS + m + 1)
                nc.gpsimd.tensor_tensor(probs[:, m % 4], probs[:, m % 4],
                                        scale_p[:, m % 4, :].unsqueeze(2).broadcast_to([P, 4, S]), ALU.mult)\
                  .then_inc(s_norm, 1)

            def h_lo(n):
                def part(it):
                    g = it - 2
                    if exists(g):
                        pool.wait_ge(taken[f"f1_{n}"], 2 * (g + 1))
                        pool.wait_ge(s_hi["f1"], 8 * g + 2 * (n + 1))
                        nc.gpsimd.tensor_tensor(hT[:, 1, 2 * n:2 * n + 2, :], h_full[:, n % 2],
                                                f32(hT[:, 0, 2 * n:2 * n + 2, :]), ALU.subtract).then_inc(s_hlo, 1)
                return part

            def residual(it):
                g = it - 1
                if exists(g):
                    pool.wait_ge(s_xres, 16 * (g + 1))
                    nc.gpsimd.tensor_tensor(x_res[:], x_res[:], row(bo_row), ALU.add).then_inc(s_xb, 1)

            def rstd1(it):
                g = it - 1
                if exists(g):
                    pool.wait_ge(s_ve1, g + 1)
                    need(pool, s_z1, GB * g)
                    nc.gpsimd.tensor_tensor(rstd[:, 0, :], var_eps[:, 0, :], neg_half[:], ALU.pow).then_inc(s_rs1, 1)

            def affine1(it):
                g = it - 1
                if exists(g):
                    pool.wait_ge(s_z1, GB * (g + 1))
                    need(pool, full["yT"], g)
                    need(pool, s_yb, g)
                    nc.gpsimd.tensor_tensor(y[:], u1[:], row(g1_row), ALU.mult).then_inc(s_y0, 1)
                    pool.wait_ge(s_y0, g + 1)
                    nc.gpsimd.tensor_tensor(y[:], y[:], row(be1_row), ALU.add).then_inc(s_y, 1)

            def add_b2(it):
                g = it - 2
                if exists(g):
                    pool.wait_ge(s_y, g + 1)
                    need(pool, taken["f2"], g)
                    nc.gpsimd.tensor_tensor(y_b2[:], y[:], row(b2_row), ALU.add).then_inc(s_yb, 1)

            def rstd2(it):
                g = it - 3
                if exists(g):
                    pool.wait_ge(s_ve2, g + 1)
                    need(pool, s_z2, GB * g)
                    nc.gpsimd.tensor_tensor(rstd[:, 1, :], var_eps[:, 1, :], neg_half[:], ALU.pow).then_inc(s_rs2, 1)

            def affine2(it):
                g = it - 3
                if exists(g):
                    pool.wait_ge(s_z2, GB * (g + 1))
                    need(pool, s_out, 16 * g)
                    nc.gpsimd.tensor_tensor(o_tok[:], u2[:], row(g2_row), ALU.mult).then_inc(s_o0, 1)
                    pool.wait_ge(s_o0, g + 1)
                    nc.gpsimd.tensor_tensor(o_tok[:], o_tok[:], row(be2_row), ALU.add).then_inc(s_o, 1)

            WORK = [[affine2, h_lo(0)], [h_lo(1), add_b2], [residual, h_lo(2)], [h_lo(3), rstd1],
                    [affine1], [], [], []]

            def iteration(it, odd):
                rstd2(it)
                for slot in range(UNITS):
                    normalise(it, slot)
                    for part in WORK[slot]:
                        part(it)

            run(pool, iteration)


_INS = ["x", "ctx_1024"] + ["L0_xattn_" + n for n in (
    "Wq", "bq", "Wk", "bk", "Wv", "bv", "Wo", "bo", "ln1_g", "ln1_b", "W1", "b1", "W2", "b2", "ln2_g", "ln2_b")]
_OUTS = [((B, S, D), "float32")]


def kernel(**inputs):
    import numpy as _np
    import concourse.bacc as _bacc
    from concourse import mybir as _mybir
    from concourse.bass_utils import run_bass_kernel_spmd as _run

    nc = _bacc.Bacc("TRN2", target_bir_lowering=False, num_devices=1)
    arrays, args = {}, []
    for name in _INS:
        a = _np.ascontiguousarray(inputs[name])
        arrays[f"in_{name}_dram"] = a
        args.append(nc.dram_tensor(f"in_{name}_dram", a.shape, _mybir.dt.from_np(a.dtype), kind="ExternalInput").ap())
    for i, (shape, dtype) in enumerate(_OUTS):
        dt = _mybir.dt.from_np(_np.dtype(dtype))
        args.append(nc.dram_tensor(f"out_{i}_dram", shape, dt, kind="ExternalOutput").ap())
    encoder_layer(nc, *args)
    r = _run(nc, [arrays], core_ids=[0])
    got = tuple(r.results[0][f"out_{i}_dram"] for i in range(len(_OUTS)))
    return got[0]
```

```python
from contextlib import ExitStack

import concourse.bass as bass
from concourse import mybir

F32 = mybir.dt.float32
F32R = mybir.dt.float32r
BF16 = mybir.dt.bfloat16
ALU = mybir.AluOpType
ACT = mybir.ActivationFunctionType
AX = mybir.AxisListType

P = 128
B, S, D = 128, 128, 256
H, DK = 16, 16
FF = 1024
KC = D // P
FC = FF // P
GB = 2
NG = B // GB
GT = GB * S
PAIRS = H // 2
UNITS = GB * 4
LN_EPS = 1e-5
MASKED = -1e30
PARTS = 3
QPART = (0, 0, 1)
KPART = (0, 1, 0)
SPLIT = ((0, 0), (0, 1), (1, 0))
FIRST, LAST = 4, NG - 3


def exists(g):
    return 0 <= g < NG if isinstance(g, int) else True


def need(eng, sem, value):
    if not isinstance(value, int) or value > 0:
        eng.wait_ge(sem, value)


def count(eng, value):
    return value if isinstance(value, int) else eng.snap(value)


def lagged(it, slot, lag):
    m = slot - lag
    return (it, m) if m >= 0 else (it - 1, m + UNITS)


def run(eng, iteration):
    for it in range(-1, FIRST):
        iteration(it, it % 2)
    with eng.Fori(FIRST, LAST, 2) as it:
        iteration(it, 0)
        iteration(it + 1, 1)
    for it in range(LAST + 1, NG + 3):
        iteration(it, it % 2)


def encoder_layer(nc, x, ctx_in, Wq, bq, Wk, bk, Wv, bv, Wo, bo, ln1_g, ln1_b, W1, b1, W2, b2, ln2_g, ln2_b, out):
    ctx = ExitStack()
    with ctx:
        def sb(name, shape, dt=F32):
            return ctx.enter_context(nc.sbuf_tensor(name, shape, dt))

        def psum(name, shape):
            return ctx.enter_context(nc.psum_tensor(name, shape, F32))

        def sem(name):
            return ctx.enter_context(nc.semaphore(name))

        x_v = x.rearrange("(g b) s d -> g s b d", b=GB)
        c_v = ctx_in.rearrange("(g b) s d -> g s b d", b=GB)
        out_v = out.rearrange("(g b) s d -> g s b d", b=GB)

        wq = sb("wq", [P, 2, KC, D], F32R)
        wk = sb("wk", [P, 2, KC, D], F32R)
        wv = sb("wv", [P, 2, KC, D], F32R)
        wo = sb("wo", [P, 2, KC, D], F32R)
        w1 = sb("w1", [P, 2, KC, FF], F32R)
        w2 = sb("w2", [P, 2, FC, D], F32R)
        bq_col = sb("bq_col", [P, KC])
        bk_col = sb("bk_col", [P, KC])
        bv_row = sb("bv_row", [P, GB, D])
        bo_row = sb("bo_row", [P, D])
        g1_row = sb("g1_row", [P, D])
        be1_row = sb("be1_row", [P, D])
        b2_row = sb("b2_row", [P, D])
        g2_row = sb("g2_row", [P, D])
        be2_row = sb("be2_row", [P, D])
        b1_split = sb("b1_split", [2, FF], F32R)
        ones2 = sb("ones2", [2, GT], F32R)
        ident = sb("ident", [P, P])
        ident_bf = sb("ident_bf", [P, P], BF16)
        mask_f = sb("mask_f", [P, P])
        mask_bf = sb("mask_bf", [P, P], BF16)
        not_first = sb("not_first", [P, 1])
        neg_half = sb("neg_half", [P, GB])
        of_head = sb("of_head", [P, 2])

        x_tok = sb("x_tok", [P, GB, D])
        c_tok = sb("c_tok", [P, GB, D])
        x_res = sb("x_res", [P, GB, D])
        xT = sb("xT", [P, 2, KC, GT], F32R)
        cT = sb("cT", [P, 2, KC, GT], F32R)
        qT = sb("qT", [P, 2, KC, GT], F32R)
        kT = sb("kT", [P, 2, KC, GT], F32R)
        k_head = sb("k_head", [P, 2, KC, 2, GT], F32R)
        q_stack = [sb(f"q_stack{i}", [PARTS * 32, 4, KC, GT], F32R) for i in range(2)]
        k_stack = [sb(f"k_stack{i}", [PARTS * 32, 4, KC, 2, GT], F32R) for i in range(2)]
        v_sb = [sb(f"v_sb{i}", [P, GB, PAIRS, 3, DK]) for i in range(2)]
        probs = sb("probs", [P, 4, 4, S])
        probsT = sb("probsT", [P, 4, 4, S])
        negmax = sb("negmax", [P, 4, 4])
        sums = sb("sums", [P, 4, 4])
        recip = sb("recip", [P, 4, 4])
        scale_p = sb("scale_p", [P, 4, 4])
        aT = sb("aT", [P, 2, KC, GT], F32R)
        u1 = sb("u1", [P, GB, D])
        y = sb("y", [P, GB, D])
        y_b2 = sb("y_b2", [P, GB, D])
        yT = sb("yT", [P, 2, KC, GT], F32R)
        hT = sb("hT", [P, 2, FC, GT], F32R)
        u2 = sb("u2", [P, GB, D])
        o_tok = sb("o_tok", [P, GB, D])
        stats = sb("stats", [P, 2, GB, 6])
        mv = sb("mv", [P, 2, GB, 2])
        var_eps = sb("var_eps", [P, 2, GB])
        rstd = sb("rstd", [P, 2, GB])

        ps_scores = [psum(f"ps_scores{i}", [P, 4, S]) for i in range(2)]
        ps_probsT = [psum(f"ps_probsT{i}", [P, 4, S]) for i in range(2)]
        ps_att = psum("ps_att", [P, 512])
        ps_dense = [psum(f"ps_dense{i}", [P, 512]) for i in range(3)]

        ORDER = ["f1_0", "f1_1", "xT", "f1_2", "cT", "q", "f1_3", "k", "wo", "v", "f2", "yT"]
        BANK = {"f1_0": 2, "f1_1": 1, "xT": 0, "f1_2": 2, "cT": 1, "q": 0, "f1_3": 2, "k": 1, "wo": 0, "v": 2,
                "f2": 0, "yT": 1}
        OFFSET = {"f1_0": -2, "f1_1": -2, "f1_2": -2, "f1_3": -2, "xT": 1, "cT": 1, "q": 1, "k": 1, "v": 1,
                  "wo": -1, "f2": -2, "yT": -1}
        full = {n: sem(f"{n}_full") for n in ORDER}
        taken = {n: sem(f"{n}_taken") for n in ORDER}
        TAKES = {"f1_0": 1, "f1_1": 1, "f1_2": 1, "f1_3": 1, "xT": 1, "cT": 1, "yT": 1, "q": 2, "k": 2,
                 "v": 1, "wo": 1, "f2": 1}

        s_w = [sem(f"weight_loaded{i}") for i in range(2)]
        s_wc = sem("columns_loaded")
        s_wr = sem("rows_loaded")
        s_wb1 = sem("b1_loaded")
        s_b1 = sem("b1_steps")
        s_wscaled = sem("wq_scaled")
        s_whi = sem("weights_hi")
        s_wlo = sem("weights_lo")
        s_zero = sem("consts_zeroed")
        s_const = sem("consts_ready")
        s_cbf = sem("consts_bf_ready")
        s_x = sem("x_loaded")
        s_c = sem("c_loaded")
        s_xres = sem("x_res_loaded")
        s_xb = sem("x_res_plus_bo")
        s_hi = {n: sem(f"{n}_hi") for n in ("xT", "cT", "q", "k", "yT", "att", "f1")}
        s_khead = sem("k_head_ready")
        s_qstack = sem("q_stacked")
        s_kstack = sem("k_stacked")
        s_scores = sem("scores_ready")
        s_max = sem("max_ready")
        s_exp = sem("exp_ready")
        s_recip = sem("recip_ready")
        s_scale = sem("scale_ready")
        s_norm = sem("probs_normalised")
        s_pT = sem("probsT_full")
        s_pTsb_a = sem("probsT_taken_act")
        s_pTsb_v = sem("probsT_taken_dve")
        s_att = sem("att_ready")
        s_att_lo = sem("att_taken")
        s_st1 = sem("stats1_ready")
        s_mv1 = sem("meanvar1_ready")
        s_ve1 = sem("var_eps1_ready")
        s_rs1 = sem("rstd1_ready")
        s_z1 = sem("z1_ready")
        s_y0 = sem("y_scaled")
        s_y = sem("y_ready")
        s_yb = sem("y_b2_ready")
        s_st2 = sem("stats2_ready")
        s_mv2 = sem("meanvar2_ready")
        s_ve2 = sem("var_eps2_ready")
        s_rs2 = sem("rstd2_ready")
        s_z2 = sem("z2_ready")
        s_o0 = sem("o_scaled")
        s_o = sem("o_ready")
        s_out = sem("out_stored")

        WEIGHTS = [(Wq, wq, KC, D), (Wk, wk, KC, D), (Wv, wv, KC, D), (Wo, wo, KC, D), (W1, w1, KC, FF),
                   (W2, w2, FC, D)]
        w_raw = [t[:].rearrange("p u h k -> p (u h k)") for t in (probs, probsT)]
        raws = [w_raw[i % 2][:, 0:c * n].rearrange("p (c n) -> p c n", c=c)
                for i, (_, _, c, n) in enumerate(WEIGHTS)]
        ROWS = [(bv, bv_row[:, b, :]) for b in range(GB)] + [
            (bo, bo_row[:]), (ln1_g, g1_row[:]), (ln1_b, be1_row[:]), (b2, b2_row[:]), (ln2_g, g2_row[:]),
            (ln2_b, be2_row[:])]
        COLS = [(bq, bq_col), (bk, bk_col)]

        def f32(ap):
            return ap.bitcast(F32)

        b1_raw = [t[0:2].rearrange("p b d -> p (b d)") for t in (u1, u2)]
        b1_lo = [t[0:2].rearrange("p b d -> p (b d)") for t in (y, y_b2)]
        b1_hi = [hT[0:2, i, 0:2, :].rearrange("p c t -> p (c t)") for i in range(2)]

        block = ctx.enter_context(nc.Block())

        @block.sync
        def _(sp):
            for dram, tile in COLS:
                sp.dma_start(tile[:], dram.rearrange("(c p) -> p c", p=P), allow_slow_non_contiguous=True).then_inc(s_wc, 16)
            for dram, tile in ROWS:
                sp.dma_start(tile, dram.rearrange("(a n) -> a n", a=1).broadcast_to([P, D])).then_inc(s_wr, 16)

            def iteration(it, odd):
                x_free = count(sp, it + 2)
                out_due = count(sp, it - 2)
                res_free = count(sp, it)
                scores_done = count(sp, it * UNITS)
                q_taken = count(sp, it * KC + 2 * KC)
                k_ready = count(sp, it * 4 + 8)
                g = it + 2
                if exists(g):
                    need(sp, full["xT"], x_free)
                    sp.dma_start(x_tok[:], x_v[g]).then_inc(s_x, 16)
                g = it + 2
                if exists(g):
                    need(sp, full["cT"], x_free)
                    sp.dma_start(c_tok[:], c_v[g]).then_inc(s_c, 16)
                g = it - 3
                if exists(g):
                    need(sp, s_o, out_due)
                    sp.dma_start(out_v[g], o_tok[:]).then_inc(s_out, 16)
                g = it + 1
                if exists(g):
                    need(sp, s_scores, scores_done)
                    need(sp, taken["q"], q_taken)
                    for s, half in enumerate(QPART):
                        for j in range(4):
                            sp.dma_start(f32(q_stack[1 - odd][32 * s:32 * s + 32, j]),
                                         f32(qT[32 * j:32 * j + 32, half])).then_inc(s_qstack, 16)
                    need(sp, s_khead, k_ready)
                    for s, half in enumerate(KPART):
                        for j in range(4):
                            sp.dma_start(f32(k_stack[1 - odd][32 * s:32 * s + 32, j]),
                                         f32(k_head[32 * j:32 * j + 32, half]))\
                              .then_inc(s_kstack, 16)
                g = it
                if exists(g):
                    need(sp, taken["wo"], res_free)
                    sp.dma_start(x_res[:], x_v[g]).then_inc(s_xres, 16)

            for i in range(2):
                sp.dma_start(b1_raw[i], b1[i * FF // 2:(i + 1) * FF // 2].rearrange("(a n) -> a n", a=1)
                             .broadcast_to([2, FF // 2])).then_inc(s_wb1, 16)
            sp.dma_start(x_tok[:], x_v[0]).then_inc(s_x, 16)
            sp.dma_start(c_tok[:], c_v[0]).then_inc(s_c, 16)
            for i, ((dram, _, c, _), raw) in enumerate(zip(WEIGHTS, raws)):
                need(sp, s_wlo, i - 1)
                sp.dma_start(raw, dram.rearrange("(c p) n -> p c n", p=P)).then_inc(s_w[i % 2], 16)
            run(sp, iteration)
            sp.wait_ge(s_out, 16 * NG)

        @block.tensor
        def _(pe):
            pe.wait_ge(s_const, 3)
            pe.wait_ge(s_cbf, 2)
            pe.wait_ge(s_wlo, len(WEIGHTS))
            pe.wait_ge(s_whi, len(WEIGHTS))
            pe.wait_ge(s_b1, 9)

            def bank_free(it, name):
                n = ORDER.index(name)
                for back in range(1, 2 * len(ORDER)):
                    i, m = (it, n - back) if back <= n else (it - 1, n - back + len(ORDER))
                    if m < 0:
                        return
                    prev = ORDER[m]
                    g = i + OFFSET[prev]
                    if BANK[prev] == BANK[name] and exists(g):
                        need(pe, taken[prev], (g + 1) * TAKES[prev])
                        return

            def transposes(it, name, src):
                bank_free(it, name)
                for c in range(KC):
                    for b in range(GB):
                        last = nc.tensor.transpose(
                            ps_dense[BANK[name]][:, c * GT + b * S:c * GT + (b + 1) * S],
                            src[:, b, c * P:(c + 1) * P], ident[:])
                last.then_inc(full[name], 1)

            def columns_product(it, name, w, acts, chunks, bias=None):
                bank_free(it, name)
                for i, ch in enumerate(chunks):
                    steps = [(kc, a, c) for kc in range(KC) for a, c in SPLIT]
                    if bias is not None:
                        nc.tensor.matmul(ps_dense[BANK[name]][:, i * GT:(i + 1) * GT],
                                         bias[:, ch * P:(ch + 1) * P], ones2[:], start=True, stop=False)
                    for n, (kc, a, c) in enumerate(steps):
                        last = nc.tensor.matmul(ps_dense[BANK[name]][:, i * GT:(i + 1) * GT],
                                                w[:, a, kc, ch * P:(ch + 1) * P], acts[:, c, kc, :],
                                                start=(n == 0 and bias is None), stop=(n == len(steps) - 1))
                last.then_inc(full[name], 1)

            def tokens_product(name, w, acts, b, kcs, total):
                for kc in kcs:
                    for n, (a, c) in enumerate(SPLIT):
                        last = nc.tensor.matmul(ps_dense[BANK[name]][:, b * D:(b + 1) * D],
                                                acts[:, a, kc, b * S:(b + 1) * S], w[:, c, kc, :],
                                                start=(kc == 0 and n == 0),
                                                stop=(kc == total - 1 and n == len(SPLIT) - 1))
                return last

            def x_transpose(it):
                g = it + 1
                if exists(g):
                    pe.wait_ge(s_x, 16 * (g + 1))
                    transposes(it, "xT", x_tok)

            def c_transpose(it):
                g = it + 1
                if exists(g):
                    pe.wait_ge(s_c, 16 * (g + 1))
                    transposes(it, "cT", c_tok)

            def y_transpose(it):
                g = it - 1
                if exists(g):
                    pe.wait_ge(s_y, g + 1)
                    transposes(it, "yT", y)

            def q_project(it):
                g = it + 1
                if exists(g):
                    pe.wait_ge(taken["xT"], g + 1)
                    columns_product(it, "q", wq, xT, range(KC))

            def k_project(it):
                g = it + 1
                if exists(g):
                    pe.wait_ge(taken["cT"], g + 1)
                    columns_product(it, "k", wk, cT, range(KC))

            def v_project(it):
                g = it + 1
                if exists(g):
                    bank_free(it, "v")
                    for b in range(GB):
                        last = tokens_product("v", wv, cT, b, range(KC), KC)
                    last.then_inc(full["v"], 1)

            def out_project(it):
                g = it - 1
                if exists(g):
                    pe.wait_ge(s_att_lo, GB * (g + 1))
                    bank_free(it, "wo")
                    for b in range(GB):
                        last = tokens_product("wo", wo, aT, b, range(KC), KC)
                    last.then_inc(full["wo"], 1)

            def ff_up(n):
                def part(it):
                    g = it - 2
                    if exists(g):
                        pe.wait_ge(taken["yT"], g + 1)
                        columns_product(it, f"f1_{n}", w1, yT, (2 * n, 2 * n + 1), b1_split)
                return part

            def ff_down(q):
                def part(it):
                    g = it - 2
                    if exists(g):
                        if q == 0:
                            bank_free(it, "f2")
                        b, half = q // 2, q % 2
                        pe.wait_ge(taken[f"f1_{2 * half}"], g + 1)
                        pe.wait_ge(taken[f"f1_{2 * half + 1}"], g + 1)
                        last = tokens_product("f2", w2, hT, b, range(4 * half, 4 * half + 4), FC)
                        if q == 3:
                            last.then_inc(full["f2"], 1)
                return part

            def scores(it, slot, odd):
                g, m = it, slot
                if not exists(g):
                    return
                b, w = m // 4, m % 4
                if m == 0:
                    pe.wait_ge(s_qstack, 16 * 4 * PARTS * (g + 1))
                    pe.wait_ge(s_kstack, 16 * 4 * PARTS * (g + 1))
                need(pe, s_exp, g * UNITS + m - 1)
                bank = ps_scores[m % 2]
                nc.tensor.matmul(bank[:], ident_bf[:], mask_bf[:].unsqueeze(1).broadcast_to([P, 4, S]),
                                 start=True, stop=False, skip_group_check=True)
                for i in range(2):
                    c, j = w // 2, 2 * (w % 2) + i
                    last = nc.tensor.matmul(bank[:, 2 * i:2 * i + 2, :], q_stack[odd][:, j, c, b * S:(b + 1) * S],
                                            k_stack[odd][:, j, c, :, b * S:(b + 1) * S], start=False, stop=(i == 1),
                                            skip_group_check=True)
                last.then_inc(s_scores, 1)

            def probs_transpose(it, slot):
                g, m = lagged(it, slot, 2)
                if not exists(g):
                    return
                pe.wait_ge(s_norm, g * UNITS + m + 1)
                need(pe, (s_pTsb_a, s_pTsb_v)[m % 2], g * (UNITS // 2) + m // 2)
                for i in range(4):
                    last = nc.tensor.transpose(ps_probsT[m % 2][:, i, :], probs[:, m % 4, i, :], ident[:])
                last.then_inc(s_pT, 1)

            def attend(it, slot, odd):
                g, m = lagged(it, slot, 3)
                parity = odd if slot >= 3 else 1 - odd
                if m % 2 == 0 or not exists(g):
                    return
                b, c = m // 4, (m % 4) // 2
                pe.wait_ge(s_pTsb_a, g * (UNITS // 2) + m // 2 + 1)
                pe.wait_ge(s_pTsb_v, g * (UNITS // 2) + m // 2 + 1)
                if m == 1:
                    pe.wait_ge(taken["v"], g + 1)
                if c == 0:
                    need(pe, s_att_lo, g * GB + b)
                for e in range(2):
                    for j in range(4):
                        unit = (m - 1 + j // 2) % 4
                        last = nc.tensor.matmul(
                            ps_att[32 * j:32 * j + 32, c * S:(c + 1) * S],
                            v_sb[parity][:, b, 4 * c + j, e:e + 2, :],
                            probsT[:, unit, 2 * (j % 2) + e, :],
                            start=(e == 0), stop=(e == 1), tile_position=(0, 32 * j), skip_group_check=True)
                last.then_inc(s_att, 1)

            DENSE = [([ff_up(0)], [ff_up(1)]),
                     ([x_transpose, ff_up(2)], [c_transpose]),
                     ([q_project], [ff_up(3)]),
                     ([k_project], []),
                     ([out_project], [v_project]),
                     ([ff_down(0)], []),
                     ([ff_down(1)], [ff_down(2)]),
                     ([y_transpose, ff_down(3)], [])]

            def iteration(it, odd):
                for slot in range(UNITS):
                    scores(it, slot, odd)
                    for part in DENSE[slot][0]:
                        part(it)
                    probs_transpose(it, slot)
                    for part in DENSE[slot][1]:
                        part(it)
                    attend(it, slot, odd)

            run(pe, iteration)

        @block.scalar
        def _(act):
            act.wait_ge(s_wc, 16 * len(COLS))
            act.wait_ge(s_wscaled, 2)

            def exponentials(it, slot):
                g, m = it, slot
                if not exists(g):
                    return
                act.wait_ge(s_max, g * UNITS + m + 1)
                need(act, s_pT, g * UNITS + m - 3)
                need(act, s_scale, g * UNITS + m - 3)
                for i in range(4):
                    last = nc.scalar.activation(probs[:, m % 4, i, :], ps_scores[m % 2][:, i, :], ACT.Exp,
                                                bias=negmax[:, m % 4, i:i + 1],
                                                accum_out=sums[:, m % 4, i:i + 1])
                last.then_inc(s_exp, 1)

            def take_probsT(it, slot):
                g, m = lagged(it, slot, 2)
                if m % 2 or not exists(g):
                    return
                act.wait_ge(s_pT, g * UNITS + m + 1)
                need(act, s_att, (g * UNITS + m) // 2 - 1 if isinstance(g, int) else g * (UNITS // 2) + m // 2 - 1)
                nc.scalar.activation(probsT[:, m % 4, :, :], ps_probsT[m % 2][:], ACT.Copy).then_inc(s_pTsb_a, 1)

            def take_hi(name, src, dst, g, reader, count):
                act.wait_ge(full[name], g + 1)
                need(act, reader, count)
                nc.scalar.activation(dst, src, ACT.Copy).then_inc(s_hi[name], 1)

            def x_hi(it):
                g = it + 1
                if exists(g):
                    take_hi("xT", ps_dense[BANK["xT"]][:], xT[:, 0].rearrange("p c t -> p (c t)"), g, full["q"], g)

            def c_hi(it):
                g = it + 1
                if exists(g):
                    take_hi("cT", ps_dense[BANK["cT"]][:], cT[:, 0].rearrange("p c t -> p (c t)"), g, full["v"], g)

            def y_hi(it):
                g = it - 1
                if exists(g):
                    take_hi("yT", ps_dense[BANK["yT"]][:], yT[:, 0].rearrange("p c t -> p (c t)"), g,
                            full["f1_3"], g)

            def qk_hi(name, dst, bias, reader, per):
                def part(it):
                    g = it + 1
                    if exists(g):
                        act.wait_ge(full[name], g + 1)
                        need(act, reader, per * g)
                        for c in range(KC):
                            nc.scalar.activation(dst[:, 0, c, :], ps_dense[BANK[name]][:, c * GT:(c + 1) * GT],
                                                 ACT.Identity, bias=bias[:, c:c + 1]).then_inc(s_hi[name], 1)
                return part

            def h_hi(n):
                def part(it):
                    g = it - 2
                    if exists(g):
                        act.wait_ge(full[f"f1_{n}"], g + 1)
                        need(act, full["f2"], g)
                        nc.scalar.activation(hT[:, 0, 2 * n:2 * n + 2, :].rearrange("p c t -> p (c t)"),
                                             ps_dense[BANK[f"f1_{n}"]][:], ACT.Relu).then_inc(s_hi["f1"], 1)
                return part

            def att_hi(it, slot):
                g, m = lagged(it, slot, 3)
                if m % 4 != 3 or not exists(g):
                    return
                b = m // 4
                act.wait_ge(s_att, (g * GB + b + 1) * 2)
                need(act, full["wo"], g)
                nc.scalar.activation(aT[:, 0, :, b * S:(b + 1) * S],
                                     ps_att[:, 0:KC * S].rearrange("p (c t) -> p c t", c=KC), ACT.Copy)\
                  .then_inc(s_hi["att"], 1)

            DENSE = [([h_hi(0)], [h_hi(1)]),
                     ([x_hi, h_hi(2)], [c_hi]),
                     ([qk_hi("q", qT, bq_col, s_qstack, 16 * 4 * PARTS)], [h_hi(3)]),
                     ([qk_hi("k", kT, bk_col, s_khead, 4)], []),
                     ([], []),
                     ([], []),
                     ([], []),
                     ([y_hi], [])]

            def iteration(it, odd):
                for slot in range(UNITS):
                    for part in DENSE[slot][0]:
                        part(it)
                    exponentials(it, slot)
                    take_probsT(it, slot)
                    for part in DENSE[slot][1]:
                        part(it)
                    att_hi(it, slot)

            run(act, iteration)

        @block.vector
        def _(dve):
            dve.wait_ge(s_wc, 16 * len(COLS))
            nc.vector.tensor_scalar(bq_col[:], bq_col[:], float(DK) ** -0.5, None, ALU.mult).then_inc(s_wscaled, 1)
            for i, ((_, w, _, _), raw) in enumerate(zip(WEIGHTS, raws)):
                dve.wait_ge(s_w[i % 2], 16 * (i // 2 + 1))
                if i == 0:
                    nc.vector.tensor_scalar(raw, raw, float(DK) ** -0.5, None, ALU.mult).then_inc(s_wscaled, 1)
                    dve.wait_ge(s_wscaled, 2)
                nc.vector.tensor_copy(w[:, 0], raw).then_inc(s_whi, 1)
                dve.wait_ge(s_whi, i + 1)
                nc.vector.tensor_tensor(w[:, 1], raw, f32(w[:, 0]), ALU.subtract).then_inc(s_wlo, 1)
            dve.wait_ge(s_const, 3)
            nc.vector.tensor_copy(ident_bf[:], ident[:]).then_inc(s_cbf, 1)
            nc.vector.tensor_copy(mask_bf[:], mask_f[:]).then_inc(s_cbf, 1)
            for e in range(2):
                nc.vector.tensor_reduce(of_head[:, e:e + 1],
                                        ident[:].rearrange("p (j e d) -> p e j d", j=4, e=2)[:, e], AX.XY, ALU.add)\
                  .then_inc(s_cbf, 1)
            dve.wait_ge(s_cbf, 4)
            dve.wait_ge(s_wb1, 32)
            for i in range(2):
                nc.vector.tensor_copy(b1_hi[i], b1_raw[i]).then_inc(s_b1, 1)
            dve.wait_ge(s_b1, 2)
            for i in range(2):
                nc.vector.tensor_tensor(b1_lo[i], b1_raw[i], f32(b1_hi[i]), ALU.subtract).then_inc(s_b1, 1)
            dve.wait_ge(s_b1, 4)
            for i in range(2):
                nc.vector.tensor_scalar(b1_lo[i], b1_lo[i], ident[0:2, 1:2], None, ALU.mult).then_inc(s_b1, 1)
            dve.wait_ge(s_b1, 6)
            for i in range(2):
                nc.vector.scalar_tensor_tensor(out=b1_split[:, i * FF // 2:(i + 1) * FF // 2], in0=f32(b1_hi[i]),
                                               scalar=ident[0:2, 0:1], in1=b1_lo[i], op0=ALU.mult,
                                               op1=ALU.add).then_inc(s_b1, 1)
            nc.vector.tensor_scalar(ones2[:], b1_raw[0][:, 0:GT], 0.0, 1.0, ALU.mult, ALU.add).then_inc(s_b1, 1)
            dve.wait_ge(s_wr, 16 * len(ROWS))

            def maxima(it, slot):
                g, m = it, slot
                if not exists(g):
                    return
                dve.wait_ge(s_scores, g * UNITS + m + 1)
                need(dve, s_exp, g * UNITS + m - 3)
                nc.vector.tensor_reduce(negmax[:, m % 4, :], ps_scores[m % 2][:], AX.X, ALU.max, negate=True)\
                  .then_inc(s_max, 1)

            def reciprocals(it, slot):
                g, m = lagged(it, slot, 1)
                if not exists(g):
                    return
                U = g * UNITS + m
                dve.wait_ge(s_exp, U + 1)
                need(dve, s_norm, U - 3)
                nc.vector.reciprocal(recip[:, m % 4, :], sums[:, m % 4, :]).then_inc(s_recip, 1)
                dve.wait_ge(s_recip, U + 1)
                nc.vector.tensor_scalar(scale_p[:, m % 4, :], recip[:, m % 4, :], not_first[:], None, ALU.mult)\
                  .then_inc(s_scale, 1)

            def take_probsT(it, slot):
                g, m = lagged(it, slot, 2)
                if m % 2 == 0 or not exists(g):
                    return
                dve.wait_ge(s_pT, g * UNITS + m + 1)
                need(dve, s_att, g * (UNITS // 2) + m // 2 - 1)
                nc.vector.tensor_copy(probsT[:, m % 4, :, :], ps_probsT[m % 2][:]).then_inc(s_pTsb_v, 1)

            def take_lo(name, src, dst, g):
                dve.wait_ge(s_hi[name], g + 1)
                nc.vector.tensor_tensor(dst[:, 1].rearrange("p c t -> p (c t)"), src,
                                        f32(dst[:, 0].rearrange("p c t -> p (c t)")), ALU.subtract)\
                  .then_inc(taken[name], 1)

            def x_lo(it):
                if exists(it + 1):
                    take_lo("xT", ps_dense[BANK["xT"]][:], xT, it + 1)

            def c_lo(it):
                if exists(it + 1):
                    take_lo("cT", ps_dense[BANK["cT"]][:], cT, it + 1)

            def y_lo(it):
                if exists(it - 1):
                    take_lo("yT", ps_dense[BANK["yT"]][:], yT, it - 1)

            def qk_lo(name, dst, bias):
                def part(it):
                    g = it + 1
                    if exists(g):
                        dve.wait_ge(s_hi[name], (g + 1) * KC)
                        for c in range(KC):
                            nc.vector.scalar_tensor_tensor(
                                out=dst[:, 1, c, :], in0=ps_dense[BANK[name]][:, c * GT:(c + 1) * GT],
                                scalar=bias[:, c:c + 1], in1=f32(dst[:, 0, c, :]), op0=ALU.add,
                                op1=ALU.subtract).then_inc(taken[name], 1)
                return part

            def k_separate(it):
                g = it + 1
                if exists(g):
                    dve.wait_ge(taken["k"], (g + 1) * KC)
                    need(dve, s_kstack, 16 * 4 * PARTS * g)
                    for half in range(2):
                        for e in range(2):
                            nc.vector.tensor_scalar(k_head[:, half, :, e, :], f32(kT[:, half]),
                                                    of_head[:, e:e + 1], None, ALU.mult).then_inc(s_khead, 1)

            def take_v(it, odd):
                g = it + 1
                if exists(g):
                    dve.wait_ge(full["v"], g + 1)
                    need(dve, s_att, (g - 1) * (UNITS // 2))
                    if isinstance(g, int) and g < 2:
                        dve.wait_ge(s_zero, 6)
                    nc.vector.tensor_tensor(
                        v_sb[1 - odd][:].rearrange("p b h e d -> p (b h) e d")[:, :, 0:3:2, :],
                        ps_dense[BANK["v"]][:].rearrange("p (b h e d) -> p (b h) e d", b=GB, h=PAIRS, e=2),
                        bv_row[:].rearrange("p b (h e d) -> p (b h) e d", h=PAIRS, e=2), ALU.add)\
                      .then_inc(taken["v"], 1)

            def h_lo(n):
                def part(it):
                    g = it - 2
                    if exists(g):
                        dve.wait_ge(s_hi["f1"], 4 * g + n + 1)
                        nc.vector.scalar_tensor_tensor(
                            out=hT[:, 1, 2 * n:2 * n + 2, :].rearrange("p c t -> p (c t)"),
                            in0=ps_dense[BANK[f"f1_{n}"]][:], scalar=0.0,
                            in1=f32(hT[:, 0, 2 * n:2 * n + 2, :]).rearrange("p c t -> p (c t)"),
                            op0=ALU.max, op1=ALU.subtract).then_inc(taken[f"f1_{n}"], 1)
                return part

            def att_lo(it, slot):
                g, m = lagged(it, slot, 3)
                if m % 4 != 3 or not exists(g):
                    return
                b = m // 4
                dve.wait_ge(s_hi["att"], g * GB + b + 1)
                nc.vector.tensor_tensor(aT[:, 1, :, b * S:(b + 1) * S],
                                        ps_att[:, 0:KC * S].rearrange("p (c t) -> p c t", c=KC),
                                        f32(aT[:, 0, :, b * S:(b + 1) * S]), ALU.subtract).then_inc(s_att_lo, 1)

            def statistics(n, u, g, s_u, s_st):
                dve.wait_ge(s_u, g + 1)
                for b in range(GB):
                    nc.vector.bn_stats(stats[:, n, b, :], u[:, b, :]).then_inc(s_st, 1)

            def mean_variance(n, g, s_mv, s_ve):
                for b in range(GB):
                    nc.vector.bn_aggr(mv[:, n, b, :], stats[:, n, b, :]).then_inc(s_mv, 1)
                dve.wait_ge(s_mv, GB * (g + 1))
                nc.vector.tensor_scalar(var_eps[:, n, :], mv[:, n, :, 1], LN_EPS, None, ALU.add).then_inc(s_ve, 1)

            def standardise(n, u, g, s_rs, s_z):
                dve.wait_ge(s_rs, g + 1)
                for b in range(GB):
                    nc.vector.tensor_scalar(u[:, b, :], u[:, b, :], mv[:, n, b, 0:1], rstd[:, n, b:b + 1],
                                            ALU.subtract, ALU.mult).then_inc(s_z, 1)

            def norm1_stats(it):
                g = it - 1
                if exists(g):
                    dve.wait_ge(full["wo"], g + 1)
                    dve.wait_ge(s_xb, g + 1)
                    need(dve, s_y0, g)
                    nc.vector.tensor_tensor(u1[:].rearrange("p b d -> p (b d)"), ps_dense[BANK["wo"]][:],
                                            x_res[:].rearrange("p b d -> p (b d)"), ALU.add)\
                      .then_inc(taken["wo"], 1)
                    statistics(0, u1, g, taken["wo"], s_st1)

            def norm1(it):
                if exists(it - 1):
                    standardise(0, u1, it - 1, s_rs1, s_z1)

            def norm2_stats(it):
                g = it - 2
                if exists(g):
                    dve.wait_ge(full["f2"], g + 1)
                    dve.wait_ge(s_yb, g + 1)
                    need(dve, s_o0, g)
                    nc.vector.tensor_tensor(u2[:].rearrange("p b d -> p (b d)"), ps_dense[BANK["f2"]][:],
                                            y_b2[:].rearrange("p b d -> p (b d)"), ALU.add)\
                      .then_inc(taken["f2"], 1)
                    statistics(1, u2, g, taken["f2"], s_st2)

            def norm2(it):
                if exists(it - 3):
                    standardise(1, u2, it - 3, s_rs2, s_z2)

            DENSE = [([norm2, h_lo(0)], [h_lo(1)]),
                     ([x_lo, h_lo(2)], [c_lo]),
                     ([qk_lo("q", qT, bq_col)], [h_lo(3)]),
                     ([qk_lo("k", kT, bk_col), k_separate], []),
                     ([norm1_stats], []),
                     ([norm1], []),
                     ([], []),
                     ([y_lo], [norm2_stats])]

            def iteration(it, odd):
                for slot in range(UNITS):
                    if slot == 0 and exists(it - 3):
                        dve.wait_ge(s_st2, GB * (it - 2))
                    if slot == 5 and exists(it - 1):
                        dve.wait_ge(s_st1, GB * it)
                    maxima(it, slot)
                    if slot == 0 and exists(it - 3):
                        mean_variance(1, it - 3, s_mv2, s_ve2)
                    if slot == 5 and exists(it - 1):
                        mean_variance(0, it - 1, s_mv1, s_ve1)
                    reciprocals(it, slot)
                    for part in DENSE[slot][0]:
                        part(it)
                    take_probsT(it, slot)
                    if slot == 4:
                        take_v(it, odd)
                    for part in DENSE[slot][1]:
                        part(it)
                    att_lo(it, slot)

            run(dve, iteration)

        @block.gpsimd
        def _(pool):
            for tile in v_sb:
                nc.gpsimd.memset(tile[:], 0.0).then_inc(s_zero, 1)
            nc.gpsimd.memset(ident[:], 0.0).then_inc(s_zero, 1)
            nc.gpsimd.memset(mask_f[:], 0.0).then_inc(s_zero, 1)
            nc.gpsimd.memset(not_first[:], 1.0).then_inc(s_zero, 1)
            nc.gpsimd.memset(neg_half[:], -0.5).then_inc(s_zero, 1)
            pool.wait_ge(s_zero, 6)
            nc.gpsimd.affine_select(out=ident[:], in_=ident[:], compare_op=ALU.not_equal, fill=1.0, base=0,
                                    pattern=[[-1, P]], channel_multiplier=1).then_inc(s_const, 1)
            nc.gpsimd.affine_select(out=mask_f[:], in_=mask_f[:], compare_op=ALU.is_gt, fill=MASKED, base=0,
                                    pattern=[[-1, P]], channel_multiplier=1).then_inc(s_const, 1)
            nc.gpsimd.affine_select(out=not_first[:], in_=not_first[:], compare_op=ALU.not_equal, fill=0.0, base=0,
                                    pattern=[[0, 1]], channel_multiplier=1).then_inc(s_const, 1)
            pool.wait_ge(s_const, 3)
            pool.wait_ge(s_wr, 16 * len(ROWS))

            def row(tile):
                return tile[:].unsqueeze(1).broadcast_to([P, GB, D])

            def normalise(it, slot):
                g, m = lagged(it, slot, 1)
                if not exists(g):
                    return
                pool.wait_ge(s_scale, g * UNITS + m + 1)
                pool.wait_ge(s_exp, g * UNITS + m + 1)
                nc.gpsimd.tensor_tensor(probs[:, m % 4], probs[:, m % 4],
                                        scale_p[:, m % 4, :].unsqueeze(2).broadcast_to([P, 4, S]), ALU.mult)\
                  .then_inc(s_norm, 1)

            def residual(it):
                g = it - 1
                if exists(g):
                    pool.wait_ge(s_xres, 16 * (g + 1))
                    nc.gpsimd.tensor_tensor(x_res[:], x_res[:], row(bo_row), ALU.add).then_inc(s_xb, 1)

            def rstd1(it):
                g = it - 1
                if exists(g):
                    pool.wait_ge(s_ve1, g + 1)
                    need(pool, s_z1, GB * g)
                    nc.gpsimd.tensor_tensor(rstd[:, 0, :], var_eps[:, 0, :], neg_half[:], ALU.pow).then_inc(s_rs1, 1)

            def affine1(it):
                g = it - 1
                if exists(g):
                    pool.wait_ge(s_z1, GB * (g + 1))
                    need(pool, full["yT"], g)
                    need(pool, s_yb, g)
                    nc.gpsimd.tensor_tensor(y[:], u1[:], row(g1_row), ALU.mult).then_inc(s_y0, 1)
                    pool.wait_ge(s_y0, g + 1)
                    nc.gpsimd.tensor_tensor(y[:], y[:], row(be1_row), ALU.add).then_inc(s_y, 1)

            def add_b2(it):
                g = it - 2
                if exists(g):
                    pool.wait_ge(s_y, g + 1)
                    need(pool, taken["f2"], g)
                    nc.gpsimd.tensor_tensor(y_b2[:], y[:], row(b2_row), ALU.add).then_inc(s_yb, 1)

            def rstd2(it):
                g = it - 3
                if exists(g):
                    pool.wait_ge(s_ve2, g + 1)
                    need(pool, s_z2, GB * g)
                    nc.gpsimd.tensor_tensor(rstd[:, 1, :], var_eps[:, 1, :], neg_half[:], ALU.pow).then_inc(s_rs2, 1)

            def affine2(it):
                g = it - 3
                if exists(g):
                    pool.wait_ge(s_z2, GB * (g + 1))
                    need(pool, s_out, 16 * g)
                    nc.gpsimd.tensor_tensor(o_tok[:], u2[:], row(g2_row), ALU.mult).then_inc(s_o0, 1)
                    pool.wait_ge(s_o0, g + 1)
                    nc.gpsimd.tensor_tensor(o_tok[:], o_tok[:], row(be2_row), ALU.add).then_inc(s_o, 1)

            WORK = [[affine2], [], [add_b2], [residual], [], [affine1], [], []]

            def iteration(it, odd):
                rstd2(it)
                for slot in range(UNITS):
                    if slot == 5:
                        rstd1(it)
                    normalise(it, slot)
                    for part in WORK[slot]:
                        part(it)

            run(pool, iteration)


_INS = ["x", "ctx_1024"] + ["L0_xattn_" + n for n in (
    "Wq", "bq", "Wk", "bk", "Wv", "bv", "Wo", "bo", "ln1_g", "ln1_b", "W1", "b1", "W2", "b2", "ln2_g", "ln2_b")]
_OUTS = [((B, S, D), "float32")]


def kernel(**inputs):
    import numpy as _np
    import concourse.bacc as _bacc
    from concourse import mybir as _mybir
    from concourse.bass_utils import run_bass_kernel_spmd as _run

    nc = _bacc.Bacc("TRN2", target_bir_lowering=False, num_devices=1)
    arrays, args = {}, []
    for name in _INS:
        a = _np.ascontiguousarray(inputs[name])
        arrays[f"in_{name}_dram"] = a
        args.append(nc.dram_tensor(f"in_{name}_dram", a.shape, _mybir.dt.from_np(a.dtype), kind="ExternalInput").ap())
    for i, (shape, dtype) in enumerate(_OUTS):
        dt = _mybir.dt.from_np(_np.dtype(dtype))
        args.append(nc.dram_tensor(f"out_{i}_dram", shape, dt, kind="ExternalOutput").ap())
    encoder_layer(nc, *args)
    r = _run(nc, [arrays], core_ids=[0])
    got = tuple(r.results[0][f"out_{i}_dram"] for i in range(len(_OUTS)))
    return got[0]
```

```python
from contextlib import ExitStack

import concourse.bass as bass
from concourse import mybir

F32 = mybir.dt.float32
F32R = mybir.dt.float32r
ALU = mybir.AluOpType
ACT = mybir.ActivationFunctionType
AX = mybir.AxisListType

P = 128
B, S, D = 128, 128, 256
H, DK = 16, 16
FF = 1024
KC = D // P
FC = FF // P
GB = 2
NG = B // GB
GT = GB * S
PAIRS = H // 2
UNITS = GB * 4
LN_EPS = 1e-5
MASKED = -1e30
PARTS = 3
QPART = (0, 0, 1)
KPART = (0, 1, 0)
SPLIT = ((0, 0), (0, 1), (1, 0))
LAG_N, LAG_T, LAG_A = 2, 3, 4
FIRST, LAST = 4, NG - 3


def exists(g):
    return 0 <= g < NG if isinstance(g, int) else True


def need(eng, sem, value):
    if not isinstance(value, int) or value > 0:
        eng.wait_ge(sem, value)


def count(eng, value):
    return value if isinstance(value, int) else eng.snap(value)


def lagged(it, slot, lag):
    m = slot - lag
    return (it, m) if m >= 0 else (it - 1, m + UNITS)


def run(eng, iteration):
    for it in range(-1, FIRST):
        iteration(it, it % 2)
    with eng.Fori(FIRST, LAST, 2) as it:
        iteration(it, 0)
        iteration(it + 1, 1)
    for it in range(LAST + 1, NG + 3):
        iteration(it, it % 2)


def encoder_layer(nc, x, ctx_in, Wq, bq, Wk, bk, Wv, bv, Wo, bo, ln1_g, ln1_b, W1, b1, W2, b2, ln2_g, ln2_b, out):
    ctx = ExitStack()
    with ctx:
        def sb(name, shape, dt=F32):
            return ctx.enter_context(nc.sbuf_tensor(name, shape, dt))

        def psum(name, shape):
            return ctx.enter_context(nc.psum_tensor(name, shape, F32))

        def sem(name):
            return ctx.enter_context(nc.semaphore(name))

        x_v = x.rearrange("(g b) s d -> g s b d", b=GB)
        c_v = ctx_in.rearrange("(g b) s d -> g s b d", b=GB)
        out_v = out.rearrange("(g b) s d -> g s b d", b=GB)

        wq = sb("wq", [P, 2, KC, D], F32R)
        wk = sb("wk", [P, 2, KC, D], F32R)
        wv = sb("wv", [P, 2, KC, D], F32R)
        wo = sb("wo", [P, 2, KC, D], F32R)
        w1 = sb("w1", [P, 2, KC, FF], F32R)
        w2 = sb("w2", [P, 2, FC, D], F32R)
        bq_col = sb("bq_col", [P, KC])
        bk_col = sb("bk_col", [P, KC])
        bv_row = sb("bv_row", [P, GB, D])
        bo_row = sb("bo_row", [P, D])
        g1_row = sb("g1_row", [P, D])
        be1_row = sb("be1_row", [P, D])
        b2_row = sb("b2_row", [P, D])
        g2_row = sb("g2_row", [P, D])
        be2_row = sb("be2_row", [P, D])
        b1_col = sb("b1_col", [P, FC])
        ident = sb("ident", [P, P])
        mask = sb("mask", [P, P])
        neg_half = sb("neg_half", [P, GB])
        of_head = sb("of_head", [P, 2])

        x_tok = sb("x_tok", [P, GB, D])
        c_tok = sb("c_tok", [P, GB, D])
        x_res = sb("x_res", [P, GB, D])
        xT = sb("xT", [P, 2, KC, GT], F32R)
        cT = sb("cT", [P, 2, KC, GT], F32R)
        qT = sb("qT", [P, 2, KC, GT], F32R)
        kT = sb("kT", [P, 2, KC, GT], F32R)
        k_head = sb("k_head", [P, 2, KC, 2, GT], F32R)
        q_stack = [sb(f"q_stack{i}", [PARTS * 32, 4, KC, GT], F32R) for i in range(2)]
        k_stack = [sb(f"k_stack{i}", [PARTS * 32, 4, KC, 2, GT], F32R) for i in range(2)]
        v_sb = [sb(f"v_sb{i}", [P, GB, PAIRS, 3, DK]) for i in range(2)]
        probs = sb("probs", [P, 4, 4, S])
        probsT = sb("probsT", [P, 4, 4, S])
        negmax = sb("negmax", [P, 4, 4])
        sums = sb("sums", [P, 4, 4])
        recip = sb("recip", [P, 4, 4])
        aT = sb("aT", [P, 2, KC, GT], F32R)
        u1 = sb("u1", [P, GB, D])
        y = sb("y", [P, GB, D])
        y_b2 = sb("y_b2", [P, GB, D])
        yT = sb("yT", [P, 2, KC, GT], F32R)
        hT = sb("hT", [P, 2, FC, GT], F32R)
        h_f32 = sb("h_f32", [P, 2, 2, GT])
        u2 = sb("u2", [P, GB, D])
        o_tok = sb("o_tok", [P, GB, D])
        stats = sb("stats", [P, 2, GB, 6])
        mv = sb("mv", [P, 2, GB, 2])
        var_eps = sb("var_eps", [P, 2, GB])
        rstd = sb("rstd", [P, 2, GB])

        ps_scores = [psum(f"ps_scores{i}", [P, 4, S]) for i in range(2)]
        ps_probsT = [psum(f"ps_probsT{i}", [P, 4, S]) for i in range(2)]
        ps_att = psum("ps_att", [P, 512])
        ps_dense = [psum(f"ps_dense{i}", [P, 512]) for i in range(3)]

        ORDER = ["xT", "yT", "v", "q", "cT", "f1_0", "k", "f1_1", "f1_2", "f1_3", "wo", "f2"]
        BANK = {"xT": 2, "yT": 1, "v": 0, "q": 2, "cT": 1, "f1_0": 0, "k": 1, "f1_1": 2, "f1_2": 0, "f1_3": 1,
                "wo": 2, "f2": 0}
        OFFSET = {"f1_0": -2, "f1_1": -2, "f1_2": -2, "f1_3": -2, "xT": 1, "cT": 1, "q": 1, "k": 1, "v": 0,
                  "wo": -1, "f2": -2, "yT": -2}
        full = {n: sem(f"{n}_full") for n in ORDER}
        taken = {n: sem(f"{n}_taken") for n in ORDER}
        TAKES = {"f1_0": 1, "f1_1": 1, "f1_2": 1, "f1_3": 1, "xT": 1, "cT": 1, "yT": 1, "q": 2, "k": 2,
                 "v": 1, "wo": 1, "f2": 1}

        s_w = [sem(f"weight_loaded{i}") for i in range(6)]
        s_wc = sem("columns_loaded")
        s_wr = sem("rows_loaded")
        s_wscaled = sem("wq_scaled")
        s_whi = sem("weights_hi")
        s_wlo = sem("weights_lo")
        s_zero = sem("consts_zeroed")
        s_const = sem("consts_ready")
        s_ofhead = sem("of_head_ready")
        s_x = sem("x_loaded")
        s_c = sem("c_loaded")
        s_xres = sem("x_res_loaded")
        s_xb = sem("x_res_plus_bo")
        s_hi = {n: sem(f"{n}_hi") for n in ("xT", "cT", "q", "k", "yT", "att", "f1")}
        s_khead = [sem(f"k_head_{half}_ready") for half in ("hi", "lo")]
        s_qstack = [sem(f"q_stacked{i}") for i in range(2)]
        s_kstack = [sem(f"k_stacked{i}") for i in range(2)]
        s_scores = sem("scores_ready")
        s_max = sem("max_ready")
        s_exp = sem("exp_ready")
        s_recip = sem("recip_ready")
        s_query0 = sem("query0_zeroed")
        s_norm = sem("probs_normalised")
        s_pT = sem("probsT_full")
        s_pTsb = sem("probsT_taken")
        s_att = sem("att_ready")
        s_att_lo = sem("att_taken")
        s_hlo = sem("h_lo_ready")
        s_st1 = sem("stats1_ready")
        s_mv1 = sem("meanvar1_ready")
        s_ve1 = sem("var_eps1_ready")
        s_rs1 = sem("rstd1_ready")
        s_z1 = sem("centred1_ready")
        s_y = sem("y_ready")
        s_yb = sem("y_b2_ready")
        s_st2 = sem("stats2_ready")
        s_mv2 = sem("meanvar2_ready")
        s_ve2 = sem("var_eps2_ready")
        s_rs2 = sem("rstd2_ready")
        s_z2 = sem("centred2_ready")
        s_o = sem("o_ready")
        s_out = sem("out_stored")

        def f32(ap):
            return ap.bitcast(F32)

        WEIGHTS = [(Wq, wq, KC, D), (Wk, wk, KC, D), (Wv, wv, KC, D), (Wo, wo, KC, D), (W1, w1, KC, FF),
                   (W2, w2, FC, D)]
        probs_raw, probsT_raw = [t[:].rearrange("p u h k -> p (u h k)") for t in (probs, probsT)]
        RAW = [[(probs_raw[:, i * KC * D:(i + 1) * KC * D].rearrange("p (c n) -> p c n", c=KC), 0, KC)]
               for i in range(4)]
        RAW += [[(probsT_raw.rearrange("p (c n) -> p c n", c=KC), 0, KC)]]
        RAW += [[(t[:], i * GB, GB) for i, t in enumerate((u1, u2, y, o_tok))]]
        ROWS = [(bv, bv_row[:, b, :]) for b in range(GB)] + [
            (bo, bo_row[:]), (ln1_g, g1_row[:]), (ln1_b, be1_row[:]), (b2, b2_row[:]), (ln2_g, g2_row[:]),
            (ln2_b, be2_row[:])]
        COLS = [(bq, bq_col), (bk, bk_col), (b1, b1_col)]

        block = ctx.enter_context(nc.Block())

        @block.sync
        def _(sp):
            def iteration(it, odd):
                x_free = count(sp, it + 2)
                out_due = count(sp, it * GB - 2 * GB)
                res_free = count(sp, it)
                scores_done = count(sp, it * UNITS)
                q_taken = count(sp, it * KC + 2 * KC)
                k_ready = count(sp, it * 2 + 4)
                g = it + 2
                if exists(g):
                    need(sp, full["xT"], x_free)
                    sp.dma_start(x_tok[:], x_v[g]).then_inc(s_x, 16)
                g = it + 2
                if exists(g):
                    need(sp, full["cT"], x_free)
                    sp.dma_start(c_tok[:], c_v[g]).then_inc(s_c, 16)
                g = it + 1
                if exists(g):
                    need(sp, s_scores, scores_done)
                    need(sp, taken["q"], q_taken)
                    for i in range(2):
                        for s, half in enumerate(QPART):
                            for j in (2 * i, 2 * i + 1):
                                sp.dma_start(f32(q_stack[1 - odd][32 * s:32 * s + 32, j]),
                                             f32(qT[32 * j:32 * j + 32, half])).then_inc(s_qstack[i], 16)
                    for i in range(2):
                        for s, half in sorted(enumerate(KPART), key=lambda part: part[1]):
                            if i == 0:
                                need(sp, s_khead[half], k_ready)
                            for j in (2 * i, 2 * i + 1):
                                sp.dma_start(f32(k_stack[1 - odd][32 * s:32 * s + 32, j]),
                                             f32(k_head[32 * j:32 * j + 32, half])).then_inc(s_kstack[i], 16)
                if isinstance(it, int) and it == -1:
                    for dram, tile in ROWS:
                        sp.dma_start(tile, dram.rearrange("(a n) -> a n", a=1).broadcast_to([P, D]))\
                          .then_inc(s_wr, 16)
                    load_weight(5)
                g = it
                if exists(g):
                    need(sp, taken["wo"], res_free)
                    sp.dma_start(x_res[:], x_v[g]).then_inc(s_xres, 16)
                g = it - 3
                if exists(g):
                    need(sp, s_o, out_due)
                    sp.dma_start(out_v[g], o_tok[:]).then_inc(s_out, 16)

            def load_weight(i):
                dram_v = WEIGHTS[i][0].rearrange("(c p) n -> p c n", p=P)
                for raw, c, n in RAW[i]:
                    sp.dma_start(raw, dram_v[:, c:c + n, :]).then_inc(s_w[i], 16)

            load_weight(0)
            sp.dma_start(x_tok[:], x_v[0]).then_inc(s_x, 16)
            sp.dma_start(c_tok[:], c_v[0]).then_inc(s_c, 16)
            load_weight(1)
            for dram, tile in COLS:
                sp.dma_start(tile[:], dram.rearrange("(c p) -> p c", p=P), allow_slow_non_contiguous=True).then_inc(s_wc, 16)
            for i in range(2, 5):
                load_weight(i)
            run(sp, iteration)
            sp.wait_ge(s_out, 16 * NG)

        @block.tensor
        def _(pe):
            pe.wait_ge(s_const, 2)

            def bank_free(it, name):
                n = ORDER.index(name)
                for back in range(1, 2 * len(ORDER)):
                    i, m = (it, n - back) if back <= n else (it - 1, n - back + len(ORDER))
                    if m < 0:
                        return
                    prev = ORDER[m]
                    g = i + OFFSET[prev]
                    if BANK[prev] == BANK[name] and exists(g):
                        need(pe, taken[prev], (g + 1) * TAKES[prev])
                        return

            def transposes(it, name, src):
                bank_free(it, name)
                for c in range(KC):
                    for b in range(GB):
                        last = nc.tensor.transpose(
                            ps_dense[BANK[name]][:, c * GT + b * S:c * GT + (b + 1) * S],
                            src[:, b, c * P:(c + 1) * P], ident[:])
                last.then_inc(full[name], 1)

            def weights_split(g, n):
                if isinstance(g, int) and g == 0:
                    pe.wait_ge(s_whi, n + 1)
                    pe.wait_ge(s_wlo, n + 1)

            def columns_product(it, name, w, acts, chunks):
                bank_free(it, name)
                for i, ch in enumerate(chunks):
                    steps = [(kc, a, c) for kc in range(KC) for a, c in SPLIT]
                    for n, (kc, a, c) in enumerate(steps):
                        last = nc.tensor.matmul(ps_dense[BANK[name]][:, i * GT:(i + 1) * GT],
                                                w[:, a, kc, ch * P:(ch + 1) * P], acts[:, c, kc, :],
                                                start=(n == 0), stop=(n == len(steps) - 1))
                last.then_inc(full[name], 1)

            def tokens_product(name, w, acts, b, kcs, total, starts=True):
                for kc in kcs:
                    for n, (a, c) in enumerate(SPLIT):
                        last = nc.tensor.matmul(ps_dense[BANK[name]][:, b * D:(b + 1) * D],
                                                acts[:, a, kc, b * S:(b + 1) * S], w[:, c, kc, :],
                                                start=(starts and kc == 0 and n == 0),
                                                stop=(kc == total - 1 and n == len(SPLIT) - 1),
                                                skip_group_check=True)
                return last

            def x_transpose(it):
                g = it + 1
                if exists(g):
                    pe.wait_ge(s_x, 16 * (g + 1))
                    transposes(it, "xT", x_tok)

            def c_transpose(it):
                g = it + 1
                if exists(g):
                    pe.wait_ge(s_c, 16 * (g + 1))
                    transposes(it, "cT", c_tok)

            def y_transpose(it):
                g = it - 2
                if exists(g):
                    pe.wait_ge(s_y, GB * (g + 1))
                    transposes(it, "yT", y)

            def q_project(it):
                g = it + 1
                if exists(g):
                    pe.wait_ge(taken["xT"], g + 1)
                    weights_split(g, 0)
                    columns_product(it, "q", wq, xT, range(KC))

            def k_project(it):
                g = it + 1
                if exists(g):
                    pe.wait_ge(taken["cT"], g + 1)
                    weights_split(g, 1)
                    columns_product(it, "k", wk, cT, range(KC))

            def v_project(it):
                g = it
                if exists(g):
                    weights_split(g, 2)
                    bank_free(it, "v")
                    for b in range(GB):
                        last = tokens_product("v", wv, cT, b, range(KC), KC)
                    last.then_inc(full["v"], 1)

            def out_project(it):
                g = it - 1
                if exists(g):
                    pe.wait_ge(s_att_lo, GB * (g + 1))
                    weights_split(g, 3)
                    bank_free(it, "wo")
                    for b in range(GB):
                        last = tokens_product("wo", wo, aT, b, range(KC), KC)
                    last.then_inc(full["wo"], 1)

            def ff_up(n):
                def part(it):
                    g = it - 2
                    if exists(g):
                        pe.wait_ge(taken["yT"], g + 1)
                        weights_split(g, 4)
                        columns_product(it, f"f1_{n}", w1, yT, (2 * n, 2 * n + 1))
                return part

            def ff_down(q):
                def part(it):
                    g = it - 2 if q < 3 else it - 3
                    if exists(g):
                        if q == 0:
                            weights_split(g, 5)
                            bank_free(it, "f2")
                        b, half = q % 2, q // 2
                        pe.wait_ge(s_hlo, 4 * g + 2 * half + 2)
                        last = tokens_product("f2", w2, hT, b, range(4 * half, 4 * half + 4), FC,
                                              starts=(b == 0))
                        if q == 3:
                            last.then_inc(full["f2"], 1)
                return part

            def scores(it, slot, odd):
                g, m = it, slot
                if not exists(g):
                    return
                b, w = m // 4, m % 4
                if m < 2:
                    pe.wait_ge(s_qstack[m], 16 * 2 * PARTS * (g + 1))
                    pe.wait_ge(s_kstack[m], 16 * 2 * PARTS * (g + 1))
                need(pe, s_exp, g * UNITS + m - 1)
                bank = ps_scores[m % 2]
                for i in range(2):
                    c, j = w // 2, 2 * (w % 2) + i
                    last = nc.tensor.matmul(bank[:, 2 * i:2 * i + 2, :], q_stack[odd][:, j, c, b * S:(b + 1) * S],
                                            k_stack[odd][:, j, c, :, b * S:(b + 1) * S], start=True, stop=True)
                last.then_inc(s_scores, 1)

            def probs_transpose(it, slot):
                g, m = lagged(it, slot, LAG_T)
                if not exists(g):
                    return
                pe.wait_ge(s_norm, g * UNITS + m + 1)
                need(pe, s_pTsb, g * UNITS + m - 1)
                for i in range(4):
                    last = nc.tensor.transpose(ps_probsT[m % 2][:, i, :], probs[:, m % 4, i, :], ident[:])
                last.then_inc(s_pT, 1)

            def attend(it, slot, odd):
                g, m = lagged(it, slot, LAG_A)
                parity = odd if slot >= LAG_A else 1 - odd
                if m % 2 == 0 or not exists(g):
                    return
                b, c = m // 4, (m % 4) // 2
                pe.wait_ge(s_pTsb, g * UNITS + m + 1)
                if m == 1:
                    pe.wait_ge(taken["v"], g + 1)
                if c == 0:
                    need(pe, s_att_lo, g * GB + b)
                for e in range(2):
                    for j in range(4):
                        unit = (m - 1 + j // 2) % 4
                        last = nc.tensor.matmul(
                            ps_att[32 * j:32 * j + 32, c * S:(c + 1) * S],
                            v_sb[parity][:, b, 4 * c + j, e:e + 2, :],
                            probsT[:, unit, 2 * (j % 2) + e, :],
                            start=(e == 0), stop=(e == 1), tile_position=(0, 32 * j), skip_group_check=True)
                last.then_inc(s_att, 1)

            DENSE = [([x_transpose, ff_down(3)], [y_transpose]),
                     ([v_project], [q_project, c_transpose]),
                     ([ff_up(0)], [k_project]),
                     ([ff_up(1)], []),
                     ([ff_up(2)], []),
                     ([ff_up(3)], [out_project]),
                     ([ff_down(0)], []),
                     ([ff_down(1)], [ff_down(2)])]

            def iteration(it, odd):
                for slot in range(UNITS):
                    scores(it, slot, odd)
                    for part in DENSE[slot][0]:
                        part(it)
                    probs_transpose(it, slot)
                    for part in DENSE[slot][1]:
                        part(it)
                    attend(it, slot, odd)

            run(pe, iteration)

        @block.scalar
        def _(act):
            def exponentials(it, slot):
                g, m = it, slot
                if not exists(g):
                    return
                act.wait_ge(s_max, g * UNITS + m + 1)
                need(act, s_pT, g * UNITS + m - 3)
                if isinstance(g, int) and g == 0 and m < 4:
                    act.wait_ge(s_wlo, 4)
                for i in range(4):
                    last = nc.scalar.activation(probs[:, m % 4, i, :], ps_scores[m % 2][:, i, :], ACT.Exp,
                                                bias=negmax[:, m % 4, i:i + 1], scale=-1.0,
                                                accum_out=sums[:, m % 4, i:i + 1])
                last.then_inc(s_exp, 1)

            def take_probsT(it, slot):
                g, m = lagged(it, slot, LAG_T)
                if not exists(g):
                    return
                act.wait_ge(s_pT, g * UNITS + m + 1)
                if isinstance(g, int) and g == 0 and m < 4:
                    act.wait_ge(s_query0, 1)
                need(act, s_att, g * (UNITS // 2) + m // 2 - 1)
                nc.scalar.activation(probsT[:, m % 4, :, 1:S], ps_probsT[m % 2][:, :, 1:S], ACT.Copy).then_inc(s_pTsb, 1)

            def take_hi(name, src, dst, g, reader, count):
                act.wait_ge(full[name], g + 1)
                need(act, reader, count)
                nc.scalar.activation(dst, src, ACT.Copy).then_inc(s_hi[name], 1)

            def x_hi(it):
                g = it + 1
                if exists(g):
                    take_hi("xT", ps_dense[BANK["xT"]][:], xT[:, 0].rearrange("p c t -> p (c t)"), g, full["q"], g)

            def c_hi(it):
                g = it + 1
                if exists(g):
                    take_hi("cT", ps_dense[BANK["cT"]][:], cT[:, 0].rearrange("p c t -> p (c t)"), g, full["v"], g)

            def y_hi(it):
                g = it - 2
                if exists(g):
                    take_hi("yT", ps_dense[BANK["yT"]][:], yT[:, 0].rearrange("p c t -> p (c t)"), g,
                            full["f1_3"], g)

            def qk_hi(name, dst, bias, readers, per):
                def part(it):
                    g = it + 1
                    if exists(g):
                        act.wait_ge(full[name], g + 1)
                        if isinstance(g, int) and g == 0:
                            act.wait_ge(s_wc, 16 * len(COLS))
                            act.wait_ge(s_wscaled, 2)
                        for reader in readers:
                            need(act, reader, per * g)
                        for c in range(KC):
                            nc.scalar.activation(dst[:, 0, c, :], ps_dense[BANK[name]][:, c * GT:(c + 1) * GT],
                                                 ACT.Identity, bias=bias[:, c:c + 1]).then_inc(s_hi[name], 1)
                return part

            def h_hi(n):
                def part(it):
                    g = it - 2
                    if exists(g):
                        act.wait_ge(full[f"f1_{n}"], g + 1)
                        need(act, full["f2"], g)
                        for i in range(2):
                            nc.scalar.activation(hT[:, 0, 2 * n + i, :],
                                                 ps_dense[BANK[f"f1_{n}"]][:, i * GT:(i + 1) * GT], ACT.Relu,
                                                 bias=b1_col[:, 2 * n + i:2 * n + i + 1]).then_inc(s_hi["f1"], 1)
                return part

            def att_hi(it, slot):
                g, m = lagged(it, slot, LAG_A)
                if m % 4 != 3 or not exists(g):
                    return
                b = m // 4
                act.wait_ge(s_att, (g * GB + b + 1) * 2)
                need(act, full["wo"], g)
                nc.scalar.activation(aT[:, 0, :, b * S:(b + 1) * S],
                                     ps_att[:, 0:KC * S].rearrange("p (c t) -> p c t", c=KC), ACT.Copy)\
                  .then_inc(s_hi["att"], 1)

            DENSE = [([x_hi], [], [y_hi]),
                     ([], [], [c_hi, qk_hi("q", qT, bq_col, s_qstack, 16 * 2 * PARTS)]),
                     ([], [h_hi(0)], [qk_hi("k", kT, bk_col, s_khead, 2)]),
                     ([], [h_hi(1)], []),
                     ([], [h_hi(2)], []),
                     ([], [h_hi(3)], []),
                     ([], [], []),
                     ([], [], [])]

            def iteration(it, odd):
                for slot in range(UNITS):
                    for part in DENSE[slot][0]:
                        part(it)
                    exponentials(it, slot)
                    for part in DENSE[slot][1]:
                        part(it)
                    take_probsT(it, slot)
                    for part in DENSE[slot][2]:
                        part(it)
                    att_hi(it, slot)

            run(act, iteration)

        @block.vector
        def _(dve):
            dve.wait_ge(s_const, 2)
            for e in range(2):
                nc.vector.tensor_reduce(of_head[:, e:e + 1],
                                        ident[:].rearrange("p (j e d) -> p e j d", j=4, e=2)[:, e], AX.XY, ALU.add)\
                  .then_inc(s_ofhead, 1)

            def split_weight(i):
                w = WEIGHTS[i][1]
                dve.wait_ge(s_w[i], 16 * len(RAW[i]))
                if i == 0:
                    raw = RAW[0][0][0]
                    nc.vector.tensor_scalar(raw, raw, float(DK) ** -0.5, None, ALU.mult).then_inc(s_wscaled, 1)
                    dve.wait_ge(s_wscaled, 1)
                for raw, c, n in RAW[i]:
                    last = nc.vector.tensor_copy(w[:, 0, c:c + n], raw)
                last.then_inc(s_whi, 1)
                dve.wait_ge(s_whi, i + 1)
                for raw, c, n in RAW[i]:
                    last = nc.vector.tensor_tensor(w[:, 1, c:c + n], raw, f32(w[:, 0, c:c + n]), ALU.subtract)
                last.then_inc(s_wlo, 1)

            dve.wait_ge(s_ofhead, 2)
            split_weight(0)

            def reciprocals(it, slot):
                g, m = lagged(it, slot, LAG_N)
                if not exists(g):
                    return
                nc.vector.reciprocal(recip[:, m % 4, :], sums[:, m % 4, :]).then_inc(s_recip, 1)

            def maxima(it, slot):
                g, m = it, slot
                if exists(g):
                    dve.wait_ge(s_scores, g * UNITS + m + 1)
                elif exists(it - 1) and slot < LAG_N:
                    dve.wait_ge(s_exp, it * UNITS)
                reciprocals(it, slot)
                if exists(g):
                    for i in range(4):
                        last = nc.vector.tensor_tensor_reduce(
                            ps_scores[m % 2][:, i, :], ps_scores[m % 2][:, i, :], mask[:], -1.0, -MASKED, ALU.add,
                            ALU.min, accum_out=negmax[:, m % 4, i:i + 1])
                    last.then_inc(s_max, 1)

            def take_lo(name, src, dst, g):
                dve.wait_ge(s_hi[name], g + 1)
                nc.vector.tensor_tensor(dst[:, 1].rearrange("p c t -> p (c t)"), src,
                                        f32(dst[:, 0].rearrange("p c t -> p (c t)")), ALU.subtract)\
                  .then_inc(taken[name], 1)

            def x_lo(it):
                if exists(it + 1):
                    take_lo("xT", ps_dense[BANK["xT"]][:], xT, it + 1)

            def c_lo(it):
                if exists(it + 1):
                    take_lo("cT", ps_dense[BANK["cT"]][:], cT, it + 1)

            def y_lo(it):
                if exists(it - 2):
                    take_lo("yT", ps_dense[BANK["yT"]][:], yT, it - 2)

            def qk_lo(name, dst, bias):
                def part(it):
                    g = it + 1
                    if exists(g):
                        dve.wait_ge(s_hi[name], (g + 1) * KC)
                        for c in range(KC):
                            nc.vector.scalar_tensor_tensor(
                                out=dst[:, 1, c, :], in0=ps_dense[BANK[name]][:, c * GT:(c + 1) * GT],
                                scalar=bias[:, c:c + 1], in1=f32(dst[:, 0, c, :]), op0=ALU.add,
                                op1=ALU.subtract).then_inc(taken[name], 1)
                return part

            def k_separate(it):
                g = it + 1
                if exists(g):
                    dve.wait_ge(taken["k"], (g + 1) * KC)
                    for i in range(2):
                        need(dve, s_kstack[i], 16 * 2 * PARTS * g)
                    for e in range(2):
                        nc.vector.tensor_scalar(k_head[:, 1, :, e, :], f32(kT[:, 1]),
                                                of_head[:, e:e + 1], None, ALU.mult).then_inc(s_khead[1], 1)

            def take_v(it, odd):
                g = it
                if exists(g):
                    dve.wait_ge(full["v"], g + 1)
                    need(dve, s_att, (g - 1) * (UNITS // 2))
                    if isinstance(g, int) and g < 2:
                        dve.wait_ge(s_zero, 5)
                    if isinstance(g, int) and g == 0:
                        dve.wait_ge(s_wr, 16 * len(ROWS))
                    nc.vector.tensor_tensor(
                        v_sb[odd][:].rearrange("p b h e d -> p (b h) e d")[:, :, 0:3:2, :],
                        ps_dense[BANK["v"]][:].rearrange("p (b h e d) -> p (b h) e d", b=GB, h=PAIRS, e=2),
                        bv_row[:].rearrange("p b (h e d) -> p (b h) e d", h=PAIRS, e=2), ALU.add)\
                      .then_inc(taken["v"], 1)

            def h_full(n):
                def part(it):
                    g = it - 2
                    if exists(g):
                        dve.wait_ge(s_hi["f1"], 2 * (4 * g + n + 1))
                        need(dve, s_hlo, 4 * g + n - 1)
                        for i in range(2):
                            last = nc.vector.tensor_scalar(
                                h_f32[:, n % 2, i, :], ps_dense[BANK[f"f1_{n}"]][:, i * GT:(i + 1) * GT],
                                b1_col[:, 2 * n + i:2 * n + i + 1], 0.0, ALU.add, ALU.max)
                        last.then_inc(taken[f"f1_{n}"], 1)
                return part

            def att_lo(it, slot):
                g, m = lagged(it, slot, LAG_A + 1)
                if m % 4 != 3 or not exists(g):
                    return
                b = m // 4
                dve.wait_ge(s_hi["att"], g * GB + b + 1)
                nc.vector.tensor_tensor(aT[:, 1, :, b * S:(b + 1) * S],
                                        ps_att[:, 0:KC * S].rearrange("p (c t) -> p c t", c=KC),
                                        f32(aT[:, 0, :, b * S:(b + 1) * S]), ALU.subtract).then_inc(s_att_lo, 1)

            def statistics(n, u, g, s_u, s_st):
                dve.wait_ge(s_u, g + 1)
                for b in range(GB):
                    nc.vector.bn_stats(stats[:, n, b, :], u[:, b, :]).then_inc(s_st, 1)

            def mean_variance(n, g, s_mv, s_ve):
                for b in range(GB):
                    nc.vector.bn_aggr(mv[:, n, b, :], stats[:, n, b, :]).then_inc(s_mv, 1)
                dve.wait_ge(s_mv, GB * (g + 1))
                nc.vector.tensor_scalar(var_eps[:, n, :], mv[:, n, :, 1], LN_EPS, None, ALU.add).then_inc(s_ve, 1)

            def centre(n, u, g, gain, s_z):
                for b in range(GB):
                    nc.vector.scalar_tensor_tensor(out=u[:, b, :], in0=u[:, b, :], scalar=mv[:, n, b, 0:1],
                                                   in1=gain[:], op0=ALU.subtract, op1=ALU.mult).then_inc(s_z, 1)

            def finish(n, u, g, offset, dst, s_rs, s_z, s_dst):
                dve.wait_ge(s_rs, g + 1)
                dve.wait_ge(s_z, GB * (g + 1))
                for b in range(GB):
                    nc.vector.scalar_tensor_tensor(out=dst[:, b, :], in0=u[:, b, :], scalar=rstd[:, n, b:b + 1],
                                                   in1=offset[:], op0=ALU.mult, op1=ALU.add).then_inc(s_dst, 1)

            def norm1_stats(it):
                g = it - 1
                if exists(g):
                    dve.wait_ge(full["wo"], g + 1)
                    dve.wait_ge(s_xb, g + 1)
                    need(dve, s_y, GB * g)
                    nc.vector.tensor_tensor(u1[:].rearrange("p b d -> p (b d)"), ps_dense[BANK["wo"]][:],
                                            x_res[:].rearrange("p b d -> p (b d)"), ALU.add)\
                      .then_inc(taken["wo"], 1)
                    statistics(0, u1, g, taken["wo"], s_st1)

            def norm1_centre(it):
                if exists(it - 1):
                    centre(0, u1, it - 1, g1_row, s_z1)

            def norm1(it):
                g = it - 2
                if exists(g):
                    need(dve, full["yT"], g)
                    need(dve, s_yb, g)
                    finish(0, u1, g, be1_row, y, s_rs1, s_z1, s_y)

            def norm2_sum(it):
                g = it - 3
                if exists(g):
                    dve.wait_ge(full["f2"], g + 1)
                    dve.wait_ge(s_yb, g + 1)
                    need(dve, s_o, GB * g)
                    nc.vector.tensor_tensor(u2[:].rearrange("p b d -> p (b d)"), ps_dense[BANK["f2"]][:],
                                            y_b2[:].rearrange("p b d -> p (b d)"), ALU.add)\
                      .then_inc(taken["f2"], 1)

            def norm2_stats(it):
                if exists(it - 3):
                    statistics(1, u2, it - 3, taken["f2"], s_st2)

            def norm2_centre(it):
                if exists(it - 3):
                    centre(1, u2, it - 3, g2_row, s_z2)

            def norm2(it):
                g = it - 3
                if exists(g):
                    need(dve, s_out, 16 * g)
                    finish(1, u2, g, be2_row, o_tok, s_rs2, s_z2, s_o)

            def aggregate(n, behind):
                def part(it):
                    if exists(it - behind):
                        mean_variance(n, it - behind, (s_mv1, s_mv2)[n], (s_ve1, s_ve2)[n])
                return part

            DENSE = [[norm1, norm2_sum, att_lo, x_lo],
                     [y_lo, norm2_stats, take_v, c_lo],
                     [aggregate(1, 3), qk_lo("q", qT, bq_col)],
                     [h_full(0), qk_lo("k", kT, bk_col), k_separate],
                     [att_lo, h_full(1), norm2_centre],
                     [h_full(2), norm2],
                     [h_full(3), norm1_stats],
                     [aggregate(0, 1), norm1_centre]]

            def iteration(it, odd):
                for slot in range(UNITS):
                    if slot == 2 and exists(it - 3):
                        dve.wait_ge(s_st2, GB * (it - 2))
                    if slot == 7 and exists(it - 1):
                        dve.wait_ge(s_st1, GB * it)
                    maxima(it, slot)
                    for part in DENSE[slot]:
                        if part is att_lo:
                            part(it, slot)
                        elif part is take_v:
                            part(it, odd)
                        else:
                            part(it)
                    if slot == 0 and isinstance(it, int) and it == -1:
                        dve.wait_ge(s_wc, 16 * len(COLS))
                        nc.vector.tensor_scalar(bq_col[:], bq_col[:], float(DK) ** -0.5, None, ALU.mult)\
                          .then_inc(s_wscaled, 1)
                        dve.wait_ge(s_wscaled, 2)
                        split_weight(1)
                    if slot == 3 and isinstance(it, int) and it == -1:
                        for i in range(2, 5):
                            split_weight(i)
                        dve.wait_ge(s_wlo, 5)
                        nc.vector.memset(probsT[:, :, :, 0:1], 0.0).then_inc(s_query0, 1)
                    if slot == 5 and isinstance(it, int) and it == 0:
                        split_weight(5)

            run(dve, iteration)

        @block.gpsimd
        def _(pool):
            nc.gpsimd.memset(ident[:], 0.0).then_inc(s_zero, 1)
            nc.gpsimd.memset(mask[:], 0.0).then_inc(s_zero, 1)
            nc.gpsimd.memset(neg_half[:], -0.5).then_inc(s_zero, 1)
            pool.wait_ge(s_zero, 3)
            nc.gpsimd.affine_select(out=ident[:], in_=ident[:], compare_op=ALU.not_equal, fill=1.0, base=0,
                                    pattern=[[-1, P]], channel_multiplier=1).then_inc(s_const, 1)
            nc.gpsimd.affine_select(out=mask[:], in_=mask[:], compare_op=ALU.is_gt, fill=MASKED, base=0,
                                    pattern=[[-1, P]], channel_multiplier=1).then_inc(s_const, 1)
            for tile in v_sb:
                nc.gpsimd.memset(tile[:], 0.0).then_inc(s_zero, 1)

            def row(tile):
                return tile[:].unsqueeze(1).broadcast_to([P, GB, D])

            def normalise(it, slot):
                g, m = lagged(it, slot, LAG_N)
                if not exists(g):
                    return
                pool.wait_ge(s_recip, g * UNITS + m + 1)
                nc.gpsimd.tensor_tensor(probs[:, m % 4], probs[:, m % 4],
                                        recip[:, m % 4, :].unsqueeze(2).broadcast_to([P, 4, S]), ALU.mult)\
                  .then_inc(s_norm, 1)

            def h_lo(n):
                def part(it):
                    g = it - 2
                    if exists(g):
                        pool.wait_ge(taken[f"f1_{n}"], g + 1)
                        need(pool, full["f2"], g)
                        nc.gpsimd.tensor_tensor(hT[:, 1, 2 * n:2 * n + 2, :], h_f32[:, n % 2],
                                                f32(hT[:, 0, 2 * n:2 * n + 2, :]), ALU.subtract).then_inc(s_hlo, 1)
                return part

            def k_separate(it):
                g = it + 1
                if exists(g):
                    pool.wait_ge(s_hi["k"], (g + 1) * KC)
                    for i in range(2):
                        need(pool, s_kstack[i], 16 * 2 * PARTS * g)
                    for e in range(2):
                        nc.gpsimd.tensor_tensor(k_head[:, 0, :, e, :], f32(kT[:, 0]),
                                                of_head[:, e:e + 1].unsqueeze(2).broadcast_to([P, KC, GT]),
                                                ALU.mult).then_inc(s_khead[0], 1)

            def residual(it):
                g = it - 1
                if exists(g):
                    if isinstance(g, int) and g == 0:
                        pool.wait_ge(s_wr, 16 * len(ROWS))
                    pool.wait_ge(s_xres, 16 * (g + 1))
                    nc.gpsimd.tensor_tensor(x_res[:], x_res[:], row(bo_row), ALU.add).then_inc(s_xb, 1)

            def rstd1(it):
                g = it - 1
                if exists(g):
                    pool.wait_ge(s_ve1, g + 1)
                    need(pool, s_y, GB * g)
                    nc.gpsimd.tensor_tensor(rstd[:, 0, :], var_eps[:, 0, :], neg_half[:], ALU.pow).then_inc(s_rs1, 1)

            def add_b2(it):
                g = it - 2
                if exists(g):
                    pool.wait_ge(s_y, GB * (g + 1))
                    need(pool, taken["f2"], g)
                    nc.gpsimd.tensor_tensor(y_b2[:], y[:], row(b2_row), ALU.add).then_inc(s_yb, 1)

            def rstd2(it):
                g = it - 3
                if exists(g):
                    pool.wait_ge(s_ve2, g + 1)
                    need(pool, s_o, GB * g)
                    nc.gpsimd.tensor_tensor(rstd[:, 1, :], var_eps[:, 1, :], neg_half[:], ALU.pow).then_inc(s_rs2, 1)

            WORK = [[residual], [], [rstd2, add_b2], [k_separate], [h_lo(0), h_lo(1)], [h_lo(2)], [h_lo(3)], [rstd1]]

            def iteration(it, odd):
                for slot in range(UNITS):
                    normalise(it, slot)
                    for part in WORK[slot]:
                        part(it)

            run(pool, iteration)


_INS = ["x", "ctx_1024"] + ["L0_xattn_" + n for n in (
    "Wq", "bq", "Wk", "bk", "Wv", "bv", "Wo", "bo", "ln1_g", "ln1_b", "W1", "b1", "W2", "b2", "ln2_g", "ln2_b")]
_OUTS = [((B, S, D), "float32")]


def kernel(**inputs):
    import numpy as _np
    import concourse.bacc as _bacc
    from concourse import mybir as _mybir
    from concourse.bass_utils import run_bass_kernel_spmd as _run

    nc = _bacc.Bacc("TRN2", target_bir_lowering=False, num_devices=1)
    arrays, args = {}, []
    for name in _INS:
        a = _np.ascontiguousarray(inputs[name])
        arrays[f"in_{name}_dram"] = a
        args.append(nc.dram_tensor(f"in_{name}_dram", a.shape, _mybir.dt.from_np(a.dtype), kind="ExternalInput").ap())
    for i, (shape, dtype) in enumerate(_OUTS):
        dt = _mybir.dt.from_np(_np.dtype(dtype))
        args.append(nc.dram_tensor(f"out_{i}_dram", shape, dt, kind="ExternalOutput").ap())
    encoder_layer(nc, *args)
    r = _run(nc, [arrays], core_ids=[0])
    got = tuple(r.results[0][f"out_{i}_dram"] for i in range(len(_OUTS)))
    return got[0]
```
